# Optimizing a Trainium2 kernel written in Bass

```python
import numpy as np
import jax
import jax.numpy as jnp

def _softmax(x, axis=-1):
    return jax.nn.softmax(x, axis=axis)

def _gelu(x):
    return jax.nn.gelu(x, approximate=True)

def _silu(x):
    return jax.nn.silu(x)

def _sigmoid(x):
    return jax.nn.sigmoid(x)

def _layernorm(x, axis=-1, eps=1e-05):
    m = jnp.mean(x, axis=axis, keepdims=True)
    v = jnp.var(x, axis=axis, keepdims=True)
    return (x - m) / jnp.sqrt(v + eps)

def _scatter_add(tgt, idx, src, axis=0):
    return tgt.at[idx].add(src)

def _segment_sum(src, seg, n):
    return jax.ops.segment_sum(src, seg, n)
kernel_name = 'mk_seq_postln_d1_jaxref_r8_eced0c'

def setup_inputs(seed: int=0):
    np.random.seed(seed)
    _w = jnp.asarray

    def _L0_attn_setup():
        import jax, jax.numpy as jnp
        import numpy as np
        import math
        B, S, DM = (1, 256, 512)
        H, HKV, HD = (32, 8, 128)
        EPS = 1e-06
        NEG_INF = -1e+30

        def _alibi_slopes(n_heads: int) -> np.ndarray:
            start = 2 ** (-2 ** (-(math.log2(n_heads) - 3)))
            return np.array([start * start ** i for i in range(n_heads)], dtype=np.float32)

        def _rmsnorm(t, w):
            tf = t.astype(jnp.float32)
            inv = jax.lax.rsqrt(jnp.mean(tf * tf, axis=-1, keepdims=True) + EPS)
            return (tf * inv * w).astype(t.dtype)
        key = jax.random.key(seed)
        ks = jax.random.split(key, 5)
        std = 0.02
        return {'x': jax.random.normal(ks[0], (B, S, DM), dtype=jnp.float32), 'Wq': jax.random.normal(ks[1], (H * HD, DM), dtype=jnp.float32) * std, 'Wk': jax.random.normal(ks[2], (HKV * HD, DM), dtype=jnp.float32) * std, 'Wv': jax.random.normal(ks[3], (HKV * HD, DM), dtype=jnp.float32) * std, 'Wo': jax.random.normal(ks[4], (H * HD, DM), dtype=jnp.float32).T * (std / math.sqrt(2 * 32)), 'q_norm_w': jnp.ones((HD,), dtype=jnp.float32), 'k_norm_w': jnp.ones((HD,), dtype=jnp.float32)}
    _L0_attn_in = _L0_attn_setup()

    def _L0_ffn_setup():
        import jax, jax.numpy as jnp
        import numpy as np
        D_MODEL = 512
        D_FF = 1376

        def _dequant_linear(x, w_int, scale):
            return jnp.einsum('bsd,fd->bsf', x, w_int.astype(x.dtype)) * scale
        key = jax.random.key(seed)
        ks = jax.random.split(key, 7)
        x = jax.random.normal(ks[0], (2, 256, D_MODEL), dtype=jnp.float32)
        gate_w = jax.random.randint(ks[1], (D_FF, D_MODEL), -127, 127, dtype=jnp.int32)
        up_w = jax.random.randint(ks[2], (D_FF, D_MODEL), -127, 127, dtype=jnp.int32)
        down_w = jax.random.randint(ks[3], (D_MODEL, D_FF), -127, 127, dtype=jnp.int32)
        gate_s = jax.random.uniform(ks[4], (D_FF,), dtype=jnp.float32) * 0.01 + 0.001
        up_s = jax.random.uniform(ks[5], (D_FF,), dtype=jnp.float32) * 0.01 + 0.001
        down_s = jax.random.uniform(ks[6], (D_MODEL,), dtype=jnp.float32) * 0.01 + 0.001
        return {'x': x, 'gate_w': gate_w, 'gate_s': gate_s, 'up_w': up_w, 'up_s': up_s, 'down_w': down_w, 'down_s': down_s}
    _L0_ffn_in = _L0_ffn_setup()
    _d = {'L0_attn_x': _L0_attn_in['x'], 'L0_attn_Wq': _L0_attn_in['Wq'], 'L0_attn_Wk': _L0_attn_in['Wk'], 'L0_attn_Wv': _L0_attn_in['Wv'], 'L0_attn_Wo': _L0_attn_in['Wo'], 'L0_attn_q_norm_w': _L0_attn_in['q_norm_w'], 'L0_attn_k_norm_w': _L0_attn_in['k_norm_w'], 'L0_ffn_gate_w': _L0_ffn_in['gate_w'], 'L0_ffn_gate_s': _L0_ffn_in['gate_s'], 'L0_ffn_up_w': _L0_ffn_in['up_w'], 'L0_ffn_up_s': _L0_ffn_in['up_s'], 'L0_ffn_down_w': _L0_ffn_in['down_w'], 'L0_ffn_down_s': _L0_ffn_in['down_s']}
    _x0 = _d['L0_attn_x']
    _d['L0_attn_x'] = jax.random.normal(jax.random.fold_in(jax.random.key(seed), 1), (2, 512, 512), dtype=_x0.dtype)
    del _x0
    return _d

def reference(L0_attn_x, L0_attn_Wq, L0_attn_Wk, L0_attn_Wv, L0_attn_Wo, L0_attn_q_norm_w, L0_attn_k_norm_w, L0_ffn_gate_w, L0_ffn_gate_s, L0_ffn_up_w, L0_ffn_up_s, L0_ffn_down_w, L0_ffn_down_s):

    def _L0_attn_ref(x, Wq, Wk, Wv, Wo, q_norm_w, k_norm_w):
        import jax, jax.numpy as jnp
        import numpy as np
        import math
        B, S, DM = (1, 256, 512)
        H, HKV, HD = (32, 8, 128)
        EPS = 1e-06
        NEG_INF = -1e+30

        def _alibi_slopes(n_heads: int) -> np.ndarray:
            start = 2 ** (-2 ** (-(math.log2(n_heads) - 3)))
            return np.array([start * start ** i for i in range(n_heads)], dtype=np.float32)

        def _rmsnorm(t, w):
            tf = t.astype(jnp.float32)
            inv = jax.lax.rsqrt(jnp.mean(tf * tf, axis=-1, keepdims=True) + EPS)
            return (tf * inv * w).astype(t.dtype)
        b, s, _ = x.shape
        G = H // HKV
        q = (x @ Wq.T).reshape(b, s, H, HD).transpose(0, 2, 1, 3)
        k = (x @ Wk.T).reshape(b, s, HKV, HD).transpose(0, 2, 1, 3)
        v = (x @ Wv.T).reshape(b, s, HKV, HD).transpose(0, 2, 1, 3)
        q = _rmsnorm(q, q_norm_w)
        k = _rmsnorm(k, k_norm_w)
        qg = q.reshape(b, HKV, G, s, HD)
        scores = jnp.einsum('bkgqd,bksd->bkgqs', qg, k) / math.sqrt(HD)
        slopes = jnp.asarray(_alibi_slopes(H)).reshape(HKV, G)
        pos = jnp.arange(s, dtype=jnp.float32)
        rel = pos[None, :] - pos[:, None]
        bias = jnp.where(rel > 0, NEG_INF, slopes[:, :, None, None] * rel)
        attn = jax.nn.softmax(scores + bias[None], axis=-1)
        out = jnp.einsum('bkgqs,bksd->bkgqd', attn, v)
        out = out.reshape(b, H, s, HD).transpose(0, 2, 1, 3).reshape(b, s, H * HD)
        return out @ Wo.T

    def _L0_ffn_ref(x, gate_w, gate_s, up_w, up_s, down_w, down_s):
        import jax, jax.numpy as jnp
        import numpy as np
        D_MODEL = 512
        D_FF = 1376

        def _dequant_linear(x, w_int, scale):
            return jnp.einsum('bsd,fd->bsf', x, w_int.astype(x.dtype)) * scale
        gate = jax.nn.silu(_dequant_linear(x, gate_w, gate_s))
        up = _dequant_linear(x, up_w, up_s)
        h = gate * up
        return _dequant_linear(h, down_w, down_s)
    x = L0_attn_x
    x = _layernorm(x + _L0_attn_ref(x, L0_attn_Wq, L0_attn_Wk, L0_attn_Wv, L0_attn_Wo, L0_attn_q_norm_w, L0_attn_k_norm_w), axis=-1)
    x = _layernorm(x + _L0_ffn_ref(x, L0_ffn_gate_w, L0_ffn_gate_s, L0_ffn_up_w, L0_ffn_up_s, L0_ffn_down_w, L0_ffn_down_s), axis=-1)
    return x

_drawn_inputs = setup_inputs


def setup_inputs(seed=0):
    import zlib

    import numpy as np

    out = dict(_drawn_inputs(seed))
    spreads = {'L0_attn_q_norm_w': (1.0, 0.2), 'L0_attn_k_norm_w': (1.0, 0.2)}
    factors = {}
    for name, (base, spread) in spreads.items():
        noise = np.random.default_rng([zlib.crc32(name.encode()), seed]).standard_normal(out[name].shape)
        drawn = base * np.exp(spread * noise) if base else spread * noise
        out[name] = jnp.asarray(drawn.astype(out[name].dtype))
    for name, factor in factors.items():
        out[name] = (out[name] * factor).astype(out[name].dtype)
    return out
```

```python
import math
from contextlib import ExitStack

import concourse.bass as bass
from concourse import mybir

F32 = mybir.dt.float32
F32R = mybir.dt.float32r
I32 = mybir.dt.int32
ALU = mybir.AluOpType
ACT = mybir.ActivationFunctionType
AX_X = mybir.AxisListType.X

P = 128
BATCH, SEQ, DM = 2, 512, 512
TOK = BATCH * SEQ
HEADS, KV_HEADS, HD = 32, 8, 128
GROUP = HEADS // KV_HEADS
DFF = 1376
NT = TOK // P
TB = SEQ // P
NC = DM // P
QW = GROUP * HD
KVW = 2 * HD
TILES = KV_HEADS * NT
FULL = DFF // P
REST = DFF - FULL * P
NF = FULL + 1
RMS_EPS, LN_EPS = 1e-6, 1e-5
SCALE = HD / math.sqrt(HD)
SLOPE0 = 2 ** (-2 ** (-(math.log2(HEADS) - 3)))
SLOPES = [SLOPE0 * SLOPE0 ** i for i in range(GROUP)]
MASKED = 1e30 * 2 ** KV_HEADS
HUGE = 3.0e38

WIDTH = [P * (i + 1) for i in range(TB)]
COL = [sum(WIDTH[:i]) for i in range(TB)]
SCORES = sum(WIDTH)
BANKS = [[0], [1, 3], [2]]
PT_COL = {0: 0, 1: SEQ, 3: SEQ + 384, 2: 2 * SEQ}
PT_WIDTH = {j: SEQ - P * j for j in range(TB)}
BANK_COL = [0, SEQ, 2 * SEQ]
BANK_WIDTH = [sum(PT_WIDTH[j] for j in bank) for bank in BANKS]


def block_kernel(nc, xT, x, wq, wkv, wo, q_norm, k_norm, gate_up, gate_up_rest, down, down_rest,
                 gate_s, gate_s_rest, up_s, up_s_rest, down_s, out):
    ctx = ExitStack()
    with ctx:
        def sem(name):
            return ctx.enter_context(nc.semaphore(name))

        def tensor(stack, name, shape, dt=F32):
            return stack.enter_context(nc.sbuf_tensor(name, shape, dt))

        h = tensor(ctx, "h", [P, NT, DM])
        ident = tensor(ctx, "ident", [P, P])
        rms_eps = tensor(ctx, "rms_eps", [P, GROUP + 1])
        minus_half = tensor(ctx, "minus_half", [P, 8])
        ln_stats = tensor(ctx, "ln_stats", [P, 2, 6])
        ln_mean_var = tensor(ctx, "ln_mean_var", [P, 2, 2])
        ln_var_eps = tensor(ctx, "ln_var_eps", [P, 2, 1])
        ln_rstd = tensor(ctx, "ln_rstd", [P, 2, 1])

        attn = ExitStack()
        stage = tensor(attn, "stage", [P, NC * (KVW + QW)])
        stage_kv, stage_q = stage[:, 0:NC * KVW], stage[:, NC * KVW:]
        wkv_hi = tensor(attn, "wkv_hi", [P, NC, KVW], F32R)
        wkv_lo = tensor(attn, "wkv_lo", [P, NC, KVW], F32R)
        wq_hi = tensor(attn, "wq_hi", [P, NC, QW], F32R)
        wq_lo = tensor(attn, "wq_lo", [P, NC, QW], F32R)
        xT_hi = tensor(attn, "xT_hi", [P, NC, TOK], F32R)
        xT_lo = tensor(attn, "xT_lo", [P, NC, TOK], F32R)
        wo_hi = tensor(attn, "wo_hi", [P, GROUP, DM], F32R)
        wo_lo = tensor(attn, "wo_lo", [P, GROUP, DM], F32R)
        qT_hi = tensor(attn, "qT_hi", [P, BATCH, GROUP, SEQ], F32R)
        qT_lo = tensor(attn, "qT_lo", [P, BATCH, GROUP, SEQ], F32R)
        kT_hi = tensor(attn, "kT_hi", [P, BATCH, SEQ], F32R)
        kT_lo = tensor(attn, "kT_lo", [P, BATCH, SEQ], F32R)
        v_hi = tensor(attn, "v_hi", [P, BATCH, TB, HD], F32R)
        v_lo = tensor(attn, "v_lo", [P, BATCH, TB, HD], F32R)
        oT_hi = tensor(attn, "oT_hi", [P, BATCH, GROUP, SEQ], F32R)
        oT_lo = tensor(attn, "oT_lo", [P, BATCH, GROUP, SEQ], F32R)
        probs = tensor(attn, "probs", [P, SCORES])
        pT_hi = tensor(attn, "pT_hi", [P, SCORES], F32R)
        pT_lo = tensor(attn, "pT_lo", [P, SCORES], F32R)
        neg_bias = tensor(attn, "neg_bias", [P, GROUP, SEQ])
        qk = tensor(attn, "qk", [P, GROUP + 1, HD])
        neg_max = tensor(attn, "neg_max", [P, TB])
        row_sum = tensor(attn, "row_sum", [P, TB])
        row_inv = tensor(attn, "row_inv", [P, TB])
        sq_sum = tensor(attn, "sq_sum", [P, GROUP + 1])
        sq_mean = tensor(attn, "sq_mean", [P, GROUP + 1])
        rstd = tensor(attn, "rstd", [P, GROUP + 1])
        norm_w = tensor(attn, "norm_w", [P, 2])
        k_scale = tensor(attn, "k_scale", [P, 1])
        attn.close()

        ffn = ExitStack()
        gu_raw = [tensor(ffn, f"gu_raw{s}", [P, 2, NC, P], I32) for s in range(2)]
        gu_rest_raw = tensor(ffn, "gu_rest_raw", [P, 2, NC, REST], I32)
        gate_scale = tensor(ffn, "gate_scale", [P, NF])
        up_scale = tensor(ffn, "up_scale", [P, NF])
        down_scale = tensor(ffn, "down_scale", [P, DM])
        gu_hi = [tensor(ffn, f"gu_hi{s}", [P, 2, NC, P], F32R) for s in range(2)]
        gu_lo = [tensor(ffn, f"gu_lo{s}", [P, 2, NC, P], F32R) for s in range(2)]
        gu_rest_hi = tensor(ffn, "gu_rest_hi", [P, 2, NC, REST], F32R)
        gu_rest_lo = tensor(ffn, "gu_rest_lo", [P, 2, NC, REST], F32R)
        hT_hi = tensor(ffn, "hT_hi", [P, NC, TOK], F32R)
        hT_lo = tensor(ffn, "hT_lo", [P, NC, TOK], F32R)
        act_hi = tensor(ffn, "act_hi", [P, NF, SEQ], F32R)
        act_lo = tensor(ffn, "act_lo", [P, NF, SEQ], F32R)
        down_raw = [tensor(ffn, f"down_raw{s}", [P, DM], I32) for s in range(2)]
        down_f = [tensor(ffn, f"down_f{s}", [P, DM]) for s in range(2)]
        down_hi = tensor(ffn, "down_hi", [P, NF, DM], F32R)
        down_lo = tensor(ffn, "down_lo", [P, NF, DM], F32R)
        silu = [tensor(ffn, f"silu{s}", [P, SEQ]) for s in range(2)]
        gated = [tensor(ffn, f"gated{s}", [P, SEQ]) for s in range(2)]
        y = [tensor(ffn, f"y{n}", [P, DM]) for n in range(TB)]
        ffn.close()

        bank = [ctx.enter_context(nc.psum_tensor(f"bank{i}", [P, 512], F32)) for i in range(8)]
        score_bank = bank[0:2]
        q_bank, kv_bank, o_bank, wo_bank = bank[2], bank[3], bank[6], bank[7]
        tr_bank = bank[4:6]

        x_in, kv_in, q_in, wo_in, norm_in = (sem(f"{n}_in") for n in ("x", "kv", "q", "wo", "norm"))
        xT_in = [sem(f"xT_in{b}") for b in range(BATCH)]
        rest_in, scales_in, y_out = (sem(n) for n in ("rest_in", "scales_in", "y_out"))
        gu_in, down_in = [sem(f"gu_in{s}") for s in range(2)], [sem(f"down_in{s}") for s in range(2)]
        consts_made = sem("consts_made")
        apart = sem("apart")
        consts, bias_ready, k_scale_ready = sem("consts"), sem("bias_ready"), sem("k_scale_ready")
        xT_hi_ready, xT_ready = sem("xT_hi_ready"), sem("xT_ready")
        kvw_hi_ready, kvw_ready = sem("kvw_hi_ready"), sem("kvw_ready")
        qw_hi_ready, qw_ready = sem("qw_hi_ready"), sem("qw_ready")
        wow_hi_ready, wow_ready = sem("wow_hi_ready"), sem("wow_ready")
        kv_done, q_done, v_hi_ready, v_ready = sem("kv_done"), sem("q_done"), sem("v_hi_ready"), sem("v_ready")
        sq_ready, sq_sum_ready, mean_ready, rstd_ready = sem("sq_ready"), sem("sq_sum_ready"), sem("mean_ready"), sem("rstd_ready")
        normed, qT_done, kT_done = sem("normed"), sem("qT_done"), sem("kT_done")
        qT_hi_ready, kT_hi_ready, qT_ready, kT_ready = sem("qT_hi_ready"), sem("kT_hi_ready"), sem("qT_ready"), sem("kT_ready")
        scores_done, biased, exp_done, inv_ready, probs_ready, probs3_ready = (
            sem(n) for n in ("scores_done", "biased", "exp_done", "inv_ready", "probs_ready", "probs3_ready"))
        pT_done, pT_hi_ready, pT_ready = sem("pT_done"), sem("pT_hi_ready"), sem("pT_ready")
        o_done, oT_hi_ready, oT_ready = sem("o_done"), sem("oT_hi_ready"), sem("oT_ready")
        wo_done, added = sem("wo_done"), sem("added")
        stats_ready, var_ready, var_eps_ready, ln_rstd_ready, ln_done = (
            sem(n) for n in ("stats_ready", "var_ready", "var_eps_ready", "ln_rstd_ready", "ln_done"))
        hT_done, hT_hi_ready, hT_ready = sem("hT_done"), sem("hT_hi_ready"), sem("hT_ready")
        gu_hi_ready, gu_ready, rest_hi_ready, rest_ready = (
            sem(n) for n in ("gu_hi_ready", "gu_ready", "rest_hi_ready", "rest_ready"))
        down_f_ready, down_hi_ready, down_ready = sem("down_f_ready"), sem("down_hi_ready"), sem("down_ready")
        gate_done, up_done, silu_ready, gated_ready = sem("gate_done"), sem("up_done"), sem("silu_ready"), sem("gated_ready")
        act_hi_ready, act_ready = sem("act_hi_ready"), sem("act_ready")
        y_done, y_scaled, y_added, y_ready = sem("y_done"), sem("y_scaled"), sem("y_added"), sem("y_ready")

        def wait(engine, semaphore, value):
            if not isinstance(value, int) or value > 0:
                engine.wait_ge(semaphore, value)

        def wait_apart(engine, semaphore, value):
            engine.wait_ge(semaphore, value)
            engine.sem_inc(apart, 1)

        def f32(ap):
            return ap.bitcast(F32)

        block = ctx.enter_context(nc.Block())

        @block.sync
        def _(sp):
            raw, src = (a.rearrange("p (c b q) -> p c b q", c=NC, b=BATCH) for a in (h[:].rearrange("p t d -> p (t d)"), xT))
            sp.dma_start(raw[:, :, 0, :], src[:, :, 0, :]).then_inc(xT_in[0], 16)
            sp.dma_start(stage_kv, wkv[0, :, :]).then_inc(kv_in, 16)
            sp.dma_start(stage_q, wq[0, :, :]).then_inc(q_in, 16)
            sp.dma_start(norm_w[:, 0:1], q_norm).then_inc(norm_in, 16)
            sp.dma_start(norm_w[:, 1:2], k_norm).then_inc(norm_in, 16)
            sp.dma_start(raw[:, :, 1, :], src[:, :, 1, :]).then_inc(xT_in[1], 16)
            sp.wait_ge(xT_ready, BATCH * NC)
            sp.dma_start(h[:], x.rearrange("(t p) d -> p t d", p=P)).then_inc(x_in, 16)
            sp.wait_ge(kvw_ready, 1)
            sp.dma_start(stage_kv, wkv[1, :, :]).then_inc(kv_in, 16)
            sp.wait_ge(qw_ready, 1)
            sp.dma_start(stage_q, wq[1, :, :]).then_inc(q_in, 16)
            with sp.Fori(0, KV_HEADS - 2) as g:
                sp.wait_ge(qw_ready, g + 2)
                sp.dma_start(stage_q, wo[bass.ds(g, 1), :, :].rearrange("g p n -> (g p) n")).then_inc(wo_in, 16)
                sp.wait_ge(kvw_ready, g + 2)
                sp.dma_start(stage_kv, wkv[bass.ds(g + 2, 1), :, :].rearrange("g p n -> (g p) n")).then_inc(kv_in, 16)
                sp.wait_ge(wow_ready, g + 1)
                sp.dma_start(stage_q, wq[bass.ds(g + 2, 1), :, :].rearrange("g p n -> (g p) n")).then_inc(q_in, 16)
            sp.wait_ge(qw_ready, KV_HEADS)
            sp.dma_start(stage_q, wo[KV_HEADS - 2, :, :]).then_inc(wo_in, 16)
            sp.wait_ge(wow_ready, KV_HEADS - 1)
            sp.dma_start(stage_q, wo[KV_HEADS - 1, :, :]).then_inc(wo_in, 16)
            sp.wait_ge(wow_ready, KV_HEADS)
            sp.wait_ge(q_done, TILES)
            sp.dma_start(gu_rest_raw[:].rearrange("p a c f -> p (a c f)"), gate_up_rest).then_inc(rest_in, 16)

            def load_pair(b, pair):
                for s in range(2):
                    wait(sp, gu_ready, FULL * b + 2 * pair + s - 1)
                    sp.dma_start(gu_raw[s][:].rearrange("p a c f -> p (a c f)"),
                                 gate_up[bass.ds(2 * pair + s, 1), :, :].rearrange("j p n -> (j p) n")).then_inc(gu_in[s], 16)

            def load_down(pair):
                for s in range(2):
                    wait(sp, down_f_ready, 2 * pair + s - 1)
                    sp.dma_start(down_raw[s][:], down[bass.ds(2 * pair + s, 1), :, :].rearrange("j p d -> (j p) d")).then_inc(down_in[s], 16)

            load_pair(0, 0)
            sp.dma_start(gate_scale[:, 0:FULL], gate_s).then_inc(scales_in, 16)
            sp.dma_start(gate_scale[0:REST, FULL:NF], gate_s_rest).then_inc(scales_in, 16)
            sp.dma_start(up_scale[:, 0:FULL], up_s).then_inc(scales_in, 16)
            sp.dma_start(up_scale[0:REST, FULL:NF], up_s_rest).then_inc(scales_in, 16)
            sp.dma_start(down_scale[:], down_s.partition_broadcast(P)).then_inc(scales_in, 16)
            sp.wait_ge(added, TILES)
            load_down(0)
            with sp.Fori(1, FULL // 2) as pair:
                load_pair(0, pair)
                load_down(pair)
            sp.wait_ge(down_f_ready, FULL - 1)
            sp.dma_start(down_raw[0][0:REST, :], down_rest).then_inc(down_in[0], 16)
            load_pair(1, 0)
            for n in range(TB):
                sp.wait_ge(y_ready, n + 1)
                sp.dma_start(out[n, :, :], y[n][:]).then_inc(y_out, 16)
            with sp.Fori(1, FULL // 2) as pair:
                load_pair(1, pair)
            for n in range(TB):
                sp.wait_ge(y_ready, TB + n + 1)
                sp.dma_start(out[TB + n, :, :], y[n][:]).then_inc(y_out, 16)
            sp.wait_ge(y_out, 16 * NT)

        LEAD = 5

        def has_tile(last, b, n):
            return not last or 4 * b + n + LEAD < NT

        def tile_row(b, n):
            return 1 - b if n < 3 else b

        @block.tensor
        def _(pe):
            def product(dst, a_hi, a_lo, b_hi, b_lo, first, last):
                nc.tensor.matmul(dst, a_hi, b_lo, start=first, stop=False)
                nc.tensor.matmul(dst, a_lo, b_hi, start=False, stop=False)
                return nc.tensor.matmul(dst, a_hi, b_hi, start=False, stop=last)

            def project_kv(dst, b, n):
                t = slice((TB * b + n) * P, (TB * b + n + 1) * P)
                for c in range(NC):
                    last = product(dst[:, 0:KVW], xT_hi[:, c, t], xT_lo[:, c, t],
                                   wkv_hi[:, c, :], wkv_lo[:, c, :], c == 0, c == NC - 1)
                last.then_inc(kv_done, 1)

            def project_q(dst, b, n):
                t = slice((TB * b + n) * P, (TB * b + n + 1) * P)
                for c in range(NC):
                    last = product(dst[:], xT_hi[:, c, t], xT_lo[:, c, t],
                                   wq_hi[:, c, :], wq_lo[:, c, :], c == 0, c == NC - 1)
                last.then_inc(q_done, 1)

            def transpose_qk(tile, k_bank):
                pe.wait_ge(normed, tile + 1)
                for i in range(GROUP):
                    last = nc.tensor.transpose(tr_bank[1][:, i * P:(i + 1) * P], qk[:, i, :], ident[:])
                last.then_inc(qT_done, 1)
                pe.wait_ge(v_ready, tile + 1)
                nc.tensor.transpose(k_bank[:, KVW:KVW + P], qk[:, GROUP, :], ident[:]).then_inc(kT_done, 1)

            def scores(k, b, n, i):
                wait(pe, biased, 4 * k + i - 1)
                q = slice(i * P, (i + 1) * P)
                product(score_bank[i % 2][:, 0:WIDTH[i]], qT_hi[:, b, n, q], qT_lo[:, b, n, q],
                        kT_hi[:, b, 0:WIDTH[i]], kT_lo[:, b, 0:WIDTH[i]], True, True).then_inc(scores_done, 1)

            def transpose_probs(which):
                for j in BANKS[which]:
                    for i in range(j, TB):
                        col = PT_COL[j] - BANK_COL[which] + (i - j) * P
                        last = nc.tensor.transpose(tr_bank[which % 2][:, col:col + P],
                                                   probs[:, COL[i] + j * P:COL[i] + (j + 1) * P], ident[:])
                last.then_inc(pT_done, 1)

            def attend(b, j):
                cols = slice(PT_COL[j], PT_COL[j] + PT_WIDTH[j])
                return product(o_bank[:, j * P:SEQ], v_hi[:, b, j, :], v_lo[:, b, j, :],
                               pT_hi[:, cols], pT_lo[:, cols], j == 0, j == 2)

            def project_out(tile, b, n, half):
                if half == 0:
                    wait(pe, added, tile)
                q = slice(n * P, (n + 1) * P)
                for i in (2 * half, 2 * half + 1):
                    last = product(wo_bank[:], oT_hi[:, b, i, q], oT_lo[:, b, i, q],
                                   wo_hi[:, i, :], wo_lo[:, i, :], i == 0, i == GROUP - 1)
                if half == 1:
                    last.then_inc(wo_done, 1)

            def group(g, first, last):
                for b in range(BATCH):
                    for n in range(GROUP):
                        k = 8 * g + 4 * b + n
                        has_next = has_tile(last, b, n)
                        has_prev = not (first and b == 0)
                        has_scores = not (last and b == 1 and n == GROUP - 1)
                        pe.wait_ge(probs_ready, 3 * k + 3)
                        pe.wait_ge(probs3_ready, k + 1)
                        wait(pe, pT_ready, 3 * k)
                        transpose_probs(0)
                        pe.wait_ge(qT_ready, k + LEAD if has_tile(last, b, n - 1) or n == 0 and b == 0 else TILES)
                        transpose_probs(1)
                        if has_next:
                            if b == 0 and n == 3:
                                pe.wait_ge(kvw_ready, g + 2)
                            pe.wait_ge(kT_ready, k + LEAD)
                            project_kv(kv_bank, tile_row(b, n), (n + 1) % TB)
                            if b == 0 and n == 3:
                                pe.wait_ge(qw_ready, g + 2)
                            pe.wait_ge(normed, k + LEAD)
                            project_q(q_bank, tile_row(b, n), (n + 1) % TB)
                        pe.wait_ge(pT_ready, 3 * k + 1)
                        transpose_probs(2)
                        if has_scores:
                            sb, sn = (b, n + 1) if n < 3 else (1 - b, 0)
                            if n == 3:
                                pe.wait_ge(qT_ready, 8 * g + 4 * b + 8)
                                pe.wait_ge(kT_ready, 8 * g + 4 * b + 8)
                            scores(k + 1, sb, sn, 0)
                            scores(k + 1, sb, sn, 1)
                        wait(pe, oT_ready, k)
                        attend(b, 0)
                        pe.wait_ge(pT_ready, 3 * k + 2)
                        attend(b, 1)
                        attend(b, 3)
                        if has_scores:
                            scores(k + 1, sb, sn, 2)
                            scores(k + 1, sb, sn, 3)
                        pe.wait_ge(pT_ready, 3 * k + 3)
                        attend(b, 2).then_inc(o_done, 1)
                        if has_prev:
                            if n == 0:
                                pe.wait_ge(oT_ready, 8 * g + 4 * b)
                                if b == 1:
                                    pe.wait_ge(wow_ready, g + 1)
                            project_out(k - 4, 1 - b, n, 0)
                        if has_next:
                            transpose_qk(k + LEAD, kv_bank)
                        if has_prev:
                            project_out(k - 4, 1 - b, n, 1)

            first_q = [q_bank, score_bank[0], score_bank[1], o_bank]
            first_kv = [kv_bank, wo_bank, tr_bank[0], kv_bank]
            pe.wait_ge(consts, 2)
            pe.wait_ge(xT_ready, NC)
            pe.wait_ge(kvw_ready, 1)
            for n in range(TB):
                if n == 3:
                    pe.wait_ge(kT_ready, 1)
                project_kv(first_kv[n], 0, n)
                if n == 0:
                    pe.wait_ge(qw_ready, 1)
                project_q(first_q[n], 0, n)
                if n > 0:
                    wait(pe, qT_ready, n - 1)
                    transpose_qk(n - 1, first_kv[n - 1])
            pe.wait_ge(qT_ready, 3)
            transpose_qk(3, first_kv[3])
            pe.wait_ge(xT_ready, BATCH * NC)
            pe.wait_ge(kT_ready, TB)
            project_kv(kv_bank, 1, 0)
            pe.wait_ge(qT_ready, TB)
            scores(0, 0, 0, 0)
            scores(0, 0, 0, 1)
            project_q(q_bank, 1, 0)
            scores(0, 0, 0, 2)
            scores(0, 0, 0, 3)
            transpose_qk(4, kv_bank)
            group(0, True, False)
            with pe.Fori(1, KV_HEADS - 1) as g:
                group(g, False, False)
            group(KV_HEADS - 1, False, True)

            def transpose_h(t):
                pe.wait_ge(ln_done, t + 1)
                wait(pe, hT_ready, t - 1)
                for c in range(NC):
                    last = nc.tensor.transpose(tr_bank[t % 2][:, c * P:(c + 1) * P], h[:, t, c * P:(c + 1) * P], ident[:])
                last.then_inc(hT_done, 1)

            pe.wait_ge(oT_ready, 8 * KV_HEADS)
            for n in range(GROUP):
                project_out(TILES - 4 + n, 1, n, 0)
                project_out(TILES - 4 + n, 1, n, 1)
                transpose_h(n)

            def hidden(b, banks, weights_hi, weights_lo, rows):
                tok = slice(SEQ * b, SEQ * (b + 1))
                for a, done in ((0, gate_done), (1, up_done)):
                    for c in range(NC):
                        last = product(banks[a][0:rows, :], weights_hi[:, a, c, :], weights_lo[:, a, c, :],
                                       hT_hi[:, c, tok], hT_lo[:, c, tok], c == 0, c == NC - 1)
                    last.then_inc(done, 1)

            def hidden_pair(b, pair):
                for s in range(2):
                    pe.wait_ge(gu_ready, FULL * b + 2 * pair + s + 1)
                    wait(pe, gated_ready, NF * b + 2 * pair + s - 1)
                    hidden(b, (bank[s], bank[2 + s]), gu_hi[s], gu_lo[s], P)

            for b in range(BATCH):
                pe.wait_ge(hT_ready, TB * b + TB)
                hidden_pair(b, 0)
                with pe.Fori(1, FULL // 2) as pair:
                    hidden_pair(b, pair)
                pe.wait_ge(rest_ready, 1)
                wait(pe, y_scaled, TB * b)
                hidden(b, bank[6:8], gu_rest_hi, gu_rest_lo, REST)
                if b == 0:
                    for n in range(TB):
                        transpose_h(TB + n)
                for n in range(TB):
                    if n == 0:
                        pe.wait_ge(down_ready, NF)
                        pe.wait_ge(act_ready, NF * b + NF)
                    if n >= 2:
                        pe.wait_ge(y_scaled, TB * b + n - 1)
                    for j in range(NF):
                        rows = P if j < FULL else REST
                        last = product(bank[6 + n % 2][:], act_hi[0:rows, j, n * P:(n + 1) * P], act_lo[0:rows, j, n * P:(n + 1) * P],
                                       down_hi[0:rows, j, :], down_lo[0:rows, j, :], j == 0, j == NF - 1)
                    last.then_inc(y_done, 1)

        @block.scalar
        def _(act):
            def hi(dst, src):
                return nc.scalar.activation(dst, src, ACT.Copy)

            def split_kv(g):
                wait(act, kv_done, 8 * g)
                act.wait_ge(kv_in, 16 * g + 16)
                hi(wkv_hi[:].rearrange("p c n -> p (c n)"), stage_kv).then_inc(kvw_hi_ready, 1)

            def split_q(g):
                wait(act, q_done, 8 * g)
                act.wait_ge(q_in, 16 * g + 16)
                hi(wq_hi[:].rearrange("p c n -> p (c n)"), stage_q).then_inc(qw_hi_ready, 1)

            def split_o(g):
                wait(act, wo_done, 8 * g)
                act.wait_ge(wo_in, 16 * g + 16)
                hi(wo_hi[:].rearrange("p c n -> p (c n)"), stage_q).then_inc(wow_hi_ready, 1)

            def tile_squares(tile, from_q, from_kv):
                wait(act, kT_done, tile)
                act.wait_ge(kv_done, tile + 1)
                nc.scalar.activation(qk[:, GROUP, :], from_kv[:, 0:HD], ACT.Square)
                act.wait_ge(q_done, tile + 1)
                nc.scalar.activation(qk[:, 0:GROUP, :].rearrange("p i d -> p (i d)"), from_q[:], ACT.Square).then_inc(sq_ready, 1)

            def tile_v(b, n, from_kv):
                hi(v_hi[:, b, n, :], from_kv[:, HD:KVW]).then_inc(v_hi_ready, 1)

            def tile_qkT(tile, b, n, from_k):
                act.wait_ge(qT_done, tile + 1)
                hi(qT_hi[:, b, :, n * P:(n + 1) * P], tr_bank[1][:].rearrange("p (i q) -> p i q", i=GROUP)).then_inc(qT_hi_ready, 1)
                act.wait_ge(kT_done, tile + 1)
                nc.scalar.activation(kT_hi[:, b, n * P:(n + 1) * P], from_k[:, KVW:KVW + P], ACT.Copy,
                                     scale=k_scale[:, 0:1]).then_inc(kT_hi_ready, 1)

            def exponentials(k, i):
                act.wait_ge(biased, 4 * k + i + 1)
                cols = probs[:, COL[i]:COL[i] + WIDTH[i]]
                nc.scalar.activation(cols, cols, ACT.Exp, bias=neg_max[:, i:i + 1], scale=-1.0,
                                     accum_out=row_sum[:, i:i + 1]).then_inc(exp_done, 1)

            def split_pT(k, which):
                act.wait_ge(pT_done, 3 * k + which + 1)
                hi(pT_hi[:, BANK_COL[which]:BANK_COL[which] + BANK_WIDTH[which]],
                   tr_bank[which % 2][:, 0:BANK_WIDTH[which]]).then_inc(pT_hi_ready, 1)

            def group(g, first, last):
                for b in range(BATCH):
                    for n in range(GROUP):
                        k = 8 * g + 4 * b + n
                        has_next = has_tile(last, b, n)
                        has_scores = not (last and b == 1 and n == GROUP - 1)
                        wait(act, o_done, k)
                        split_pT(k, 0)
                        split_pT(k, 1)
                        if has_next:
                            tile_squares(k + LEAD, q_bank, kv_bank)
                        split_pT(k, 2)
                        if has_next and n < 3:
                            tile_v(tile_row(b, n), (n + 1) % TB, kv_bank)
                        if has_scores:
                            for i in range(3):
                                exponentials(k + 1, i)
                        act.wait_ge(o_done, k + 1)
                        if has_next and n == 3:
                            tile_v(tile_row(b, n), (n + 1) % TB, kv_bank)
                        hi(oT_hi[:, b, n, :], o_bank[:]).then_inc(oT_hi_ready, 1)
                        if has_scores:
                            exponentials(k + 1, 3)
                        if b == 0 and n == 2 and not last:
                            split_kv(g + 1)
                        if has_next:
                            tile_qkT(k + LEAD, tile_row(b, n), (n + 1) % TB, kv_bank)
                        if b == 0 and n == 2 and not last:
                            split_q(g + 1)
                        if b == 0 and n == 3:
                            split_o(g)

            first_q = [q_bank, score_bank[0], score_bank[1], o_bank, q_bank]
            first_kv = [kv_bank, wo_bank, tr_bank[0], kv_bank, kv_bank]
            raw = h[:].rearrange("p t d -> p (t d)").rearrange("p (c b q) -> p c b q", c=NC, b=BATCH)
            act.wait_ge(xT_in[0], 16)
            for c in range(NC):
                hi(xT_hi[:, c, 0:SEQ], raw[:, c, 0, :]).then_inc(xT_hi_ready, 1)
            split_kv(0)
            split_q(0)
            act.wait_ge(xT_in[1], 16)
            for c in range(NC):
                hi(xT_hi[:, c, SEQ:TOK], raw[:, c, 1, :]).then_inc(xT_hi_ready, 1)
            act.wait_ge(k_scale_ready, 1)
            for n in range(TB):
                tile_squares(n, first_q[n], first_kv[n])
                tile_v(0, n, first_kv[n])
                tile_qkT(n, 0, n, first_kv[n])
            exponentials(0, 0)
            exponentials(0, 1)
            tile_squares(TB, q_bank, kv_bank)
            tile_v(1, 0, kv_bank)
            exponentials(0, 2)
            exponentials(0, 3)
            tile_qkT(TB, 1, 0, kv_bank)
            group(0, True, False)
            with act.Fori(1, KV_HEADS - 1) as g:
                group(g, False, False)
            group(KV_HEADS - 1, False, True)

            def split_gu(b, pair, s):
                j = 2 * pair + s
                act.wait_ge(gu_in[s], 16 * (FULL // 2 * b + pair + 1))
                wait(act, up_done, NF * b + j - 1)
                hi(gu_hi[s][:], gu_raw[s][:]).then_inc(gu_hi_ready, 1)

            def split_h(t):
                act.wait_ge(hT_done, t + 1)
                hi(hT_hi[:, :, t * P:(t + 1) * P], tr_bank[t % 2][:].rearrange("p (c q) -> p c q", c=NC)).then_inc(hT_hi_ready, 1)

            def hidden(b, j, s, gate_bank, rows):
                chunk = NF * b + j
                act.wait_ge(gate_done, chunk + 1)
                nc.scalar.activation(silu[s][0:rows, :], gate_bank[0:rows, :], ACT.Silu,
                                     scale=gate_scale[0:rows, bass.ds(j, 1)]).then_inc(silu_ready, 1)
                act.wait_ge(gated_ready, chunk + 1)
                hi(act_hi[0:rows, bass.ds(j, 1), :].rearrange("p j q -> p (j q)"), gated[s][0:rows, :]).then_inc(act_hi_ready, 1)

            def hidden_pair(b, pair):
                split_gu(b, pair, 1)
                hidden(b, 2 * pair, 0, bank[0], P)
                split_gu(b, pair + 1, 0)
                hidden(b, 2 * pair + 1, 1, bank[1], P)

            split_gu(0, 0, 0)
            act.wait_ge(rest_in, 16)
            hi(gu_rest_hi[:], gu_rest_raw[:]).then_inc(rest_hi_ready, 1)
            for t in range(TB):
                split_h(t)
            act.wait_ge(scales_in, 16 * 5)
            for b in range(BATCH):
                if b > 0:
                    split_gu(b, 0, 0)
                hidden_pair(b, 0)
                with act.Fori(1, FULL // 2 - 1) as pair:
                    hidden_pair(b, pair)
                split_gu(b, FULL // 2 - 1, 1)
                hidden(b, FULL - 2, 0, bank[0], P)
                hidden(b, FULL - 1, 1, bank[1], P)
                hidden(b, FULL, 0, bank[6], REST)
                if b == 0:
                    for n in range(TB):
                        split_h(TB + n)

        @block.vector
        def _(dve):
            def lo(dst, src, hi):
                return nc.vector.tensor_tensor(dst, src, f32(hi), ALU.subtract)

            def tile_squares(tile):
                dve.wait_ge(sq_ready, tile + 1)
                nc.vector.tensor_reduce(sq_sum[:], qk[:], AX_X, ALU.add).then_inc(sq_sum_ready, 1)

            def tile_norm(tile, b, n, from_q, from_kv):
                dve.wait_ge(rstd_ready, tile + 1)
                nc.vector.tensor_tensor(qk[:, 0:GROUP, :], from_q[:].rearrange("p (i d) -> p i d", i=GROUP),
                                        rstd[:, 0:GROUP].unsqueeze(2).broadcast_to([P, GROUP, HD]), ALU.mult)
                dve.wait_ge(v_hi_ready, tile + 1)
                nc.vector.tensor_scalar(qk[:, GROUP, :], from_kv[:, 0:HD], rstd[:, GROUP:GROUP + 1], None,
                                        ALU.mult).then_inc(normed, 1)
                lo(v_lo[:, b, n, :], from_kv[:, HD:KVW], v_hi[:, b, n, :]).then_inc(v_ready, 1)

            def tile_qkT(tile, b, n, from_k):
                dve.wait_ge(qT_hi_ready, tile + 1)
                q = slice(n * P, (n + 1) * P)
                lo(qT_lo[:, b, :, q], tr_bank[1][:].rearrange("p (i q) -> p i q", i=GROUP), qT_hi[:, b, :, q]).then_inc(qT_ready, 1)
                dve.wait_ge(kT_hi_ready, tile + 1)
                nc.vector.scalar_tensor_tensor(kT_lo[:, b, q], from_k[:, KVW:KVW + P], k_scale[:, 0:1], f32(kT_hi[:, b, q]),
                                               ALU.mult, ALU.subtract).then_inc(kT_ready, 1)

            def add_bias(k, n, i):
                wait_apart(dve, scores_done, 4 * k + i + 1)
                nc.vector.tensor_tensor_reduce(out=probs[:, COL[i]:COL[i] + WIDTH[i]], in0=score_bank[i % 2][:, 0:WIDTH[i]],
                                               in1=neg_bias[:, n, SEQ - WIDTH[i]:SEQ], scale=1.0, scalar=HUGE,
                                               op0=ALU.add, op1=ALU.min, accum_out=neg_max[:, i:i + 1]).then_inc(biased, 1)

            def invert(k, half):
                dve.wait_ge(exp_done, 4 * k + 2 * half + 2)
                two = slice(2 * half, 2 * half + 2)
                nc.vector.reciprocal(row_inv[:, two], row_sum[:, two]).then_inc(inv_ready, 1)

            def norm_widest(k):
                dve.wait_ge(inv_ready, 2 * k + 2)
                cols = probs[:, COL[3]:COL[3] + WIDTH[3]]
                nc.vector.tensor_scalar(cols, cols, row_inv[:, 3:4], None, ALU.mult).then_inc(probs3_ready, 1)

            def split_q(g):
                dve.wait_ge(qw_hi_ready, g + 1)
                lo(wq_lo[:].rearrange("p c n -> p (c n)"), stage_q,
                   wq_hi[:].rearrange("p c n -> p (c n)")).then_inc(qw_ready, 1)

            def add_attention(tile, t):
                dve.wait_ge(wo_done, tile + 1)
                nc.vector.tensor_tensor(h[:, t, :], wo_bank[:], h[:, t, :], ALU.add).then_inc(added, 1)

            def split_pT(k, which):
                dve.wait_ge(pT_hi_ready, 3 * k + which + 1)
                cols = slice(BANK_COL[which], BANK_COL[which] + BANK_WIDTH[which])
                lo(pT_lo[:, cols], tr_bank[which % 2][:, 0:BANK_WIDTH[which]], pT_hi[:, cols]).then_inc(pT_ready, 1)

            def statistics(tile, s, src):
                nc.vector.bn_stats(ln_stats[:, s, :], src).then_inc(stats_ready, 1)
                dve.wait_ge(stats_ready, tile + 1)
                nc.vector.bn_aggr(ln_mean_var[:, s, :], ln_stats[:, s, :]).then_inc(var_ready, 1)

            def normalize(tile, s, dst, src):
                dve.wait_ge(ln_rstd_ready, tile + 1)
                return nc.vector.tensor_scalar(dst, src, ln_mean_var[:, s, 0:1], ln_rstd[:, s, :], ALU.subtract, ALU.mult)

            def h_statistics(t):
                dve.wait_ge(added, TILES - NT + t + 1)
                statistics(t, t % 2, h[:, t, :])

            def h_normalize(t):
                normalize(t, t % 2, h[:, t, :], h[:, t, :]).then_inc(ln_done, 1)

            def group(g, first, last):
                for b in range(BATCH):
                    for n in range(GROUP):
                        k = 8 * g + 4 * b + n
                        has_next = has_tile(last, b, n)
                        has_prev = not (first and b == 0)
                        has_scores = not (last and b == 1 and n == GROUP - 1)
                        split_pT(k, 0)
                        split_pT(k, 1)
                        if has_next:
                            tile_squares(k + LEAD)
                        split_pT(k, 2)
                        if has_scores:
                            sn = (n + 1) % GROUP
                            if b == 1 and n == 3:
                                dve.wait_ge(bias_ready, 4 * g + 5)
                            elif b == 0 and n < 3:
                                dve.wait_ge(bias_ready, 4 * g + n + 2)
                            dve.wait_ge(pT_done, 3 * k + 3)
                            add_bias(k + 1, sn, 0)
                            add_bias(k + 1, sn, 1)
                            add_bias(k + 1, sn, 2)
                            invert(k + 1, 0)
                        if has_next:
                            tile_norm(k + LEAD, tile_row(b, n), (n + 1) % TB, q_bank, kv_bank)
                        if has_scores:
                            add_bias(k + 1, sn, 3)
                        dve.wait_ge(oT_hi_ready, k + 1)
                        lo(oT_lo[:, b, n, :], o_bank[:], oT_hi[:, b, n, :]).then_inc(oT_ready, 1)
                        if has_scores:
                            invert(k + 1, 1)
                            norm_widest(k + 1)
                        if has_next:
                            tile_qkT(k + LEAD, tile_row(b, n), (n + 1) % TB, kv_bank)
                        if b == 0 and n == 2 and not last:
                            split_q(g + 1)
                        if has_prev:
                            add_attention(k - 4, TB * (1 - b) + n)
                        if last and b == 1:
                            h_statistics(n)
                            if n > 0:
                                h_normalize(n - 1)

            first_q = [q_bank, score_bank[0], score_bank[1], o_bank]
            first_kv = [kv_bank, wo_bank, tr_bank[0], kv_bank]
            raw = h[:].rearrange("p t d -> p (t d)").rearrange("p (c b q) -> p c b q", c=NC, b=BATCH)
            for b in range(BATCH):
                for c in range(NC):
                    dve.wait_ge(xT_hi_ready, NC * b + c + 1)
                    tok = slice(SEQ * b, SEQ * (b + 1))
                    lo(xT_lo[:, c, tok], raw[:, c, b, :], xT_hi[:, c, tok]).then_inc(xT_ready, 1)
                if b == 0:
                    dve.wait_ge(norm_in, 32)
                    nc.vector.scalar_tensor_tensor(k_scale[:], norm_w[:, 0:1], -SCALE, norm_w[:, 1:2],
                                                   ALU.mult, ALU.mult).then_inc(k_scale_ready, 1)
            dve.wait_ge(k_scale_ready, 1)
            for n in range(TB):
                tile_squares(n)
                tile_norm(n, 0, n, first_q[n], first_kv[n])
                tile_qkT(n, 0, n, first_kv[n])
            dve.wait_ge(bias_ready, GROUP)
            add_bias(0, 0, 0)
            add_bias(0, 0, 1)
            tile_squares(TB)
            invert(0, 0)
            add_bias(0, 0, 2)
            add_bias(0, 0, 3)
            tile_norm(TB, 1, 0, q_bank, kv_bank)
            invert(0, 1)
            norm_widest(0)
            tile_qkT(TB, 1, 0, kv_bank)
            dve.wait_ge(x_in, 16)
            group(0, True, False)
            with dve.Fori(1, KV_HEADS - 1) as g:
                group(g, False, False)
            group(KV_HEADS - 1, False, True)

            def split_gu(b, j, s):
                dve.wait_ge(gu_hi_ready, FULL * b + j + 1)
                lo(gu_lo[s][:].rearrange("p a c f -> p (a c f)"), gu_raw[s][:].rearrange("p a c f -> p (a c f)"),
                   gu_hi[s][:].rearrange("p a c f -> p (a c f)")).then_inc(gu_ready, 1)

            def split_h(t):
                dve.wait_ge(hT_hi_ready, t + 1)
                tok = slice(t * P, (t + 1) * P)
                lo(hT_lo[:, :, tok], tr_bank[t % 2][:].rearrange("p (c q) -> p c q", c=NC), hT_hi[:, :, tok]).then_inc(hT_ready, 1)

            def hidden(b, j, s, up_bank, rows):
                chunk = NF * b + j
                dve.wait_ge(silu_ready, chunk + 1)
                dve.wait_ge(up_done, chunk + 1)
                nc.vector.scalar_tensor_tensor(gated[s][0:rows, :], up_bank[0:rows, :], up_scale[0:rows, bass.ds(j, 1)],
                                               silu[s][0:rows, :], ALU.mult, ALU.mult).then_inc(gated_ready, 1)
                dve.wait_ge(act_hi_ready, chunk + 1)
                part = bass.ds(j, 1)
                lo(act_lo[0:rows, part, :].rearrange("p j q -> p (j q)"), gated[s][0:rows, :],
                   act_hi[0:rows, part, :].rearrange("p j q -> p (j q)")).then_inc(act_ready, 1)

            def hidden_pair(b, pair):
                split_gu(b, 2 * pair + 1, 1)
                hidden(b, 2 * pair, 0, bank[2], P)
                split_gu(b, 2 * pair + 2, 0)
                hidden(b, 2 * pair + 1, 1, bank[3], P)

            h_normalize(TB - 1)
            split_gu(0, 0, 0)
            dve.wait_ge(rest_hi_ready, 1)
            lo(gu_rest_lo[:].rearrange("p a c f -> p (a c f)"), gu_rest_raw[:].rearrange("p a c f -> p (a c f)"),
               gu_rest_hi[:].rearrange("p a c f -> p (a c f)")).then_inc(rest_ready, 1)
            for n in range(GROUP):
                add_attention(TILES - 4 + n, TB + n)
                split_h(n)
            for n in range(TB):
                h_statistics(TB + n)
                if n > 0:
                    h_normalize(TB + n - 1)
            h_normalize(NT - 1)
            dve.wait_ge(scales_in, 16 * 5)
            for b in range(BATCH):
                if b > 0:
                    split_gu(b, 0, 0)
                hidden_pair(b, 0)
                with dve.Fori(1, FULL // 2 - 1) as pair:
                    hidden_pair(b, pair)
                split_gu(b, FULL - 1, 1)
                hidden(b, FULL - 2, 0, bank[2], P)
                hidden(b, FULL - 1, 1, bank[3], P)
                hidden(b, FULL, 0, bank[7], REST)
                if b == 0:
                    for n in range(TB):
                        split_h(TB + n)
                else:
                    dve.wait_ge(y_out, 16 * TB)
                for n in range(TB):
                    tile = TB * b + n
                    dve.wait_ge(y_done, tile + 1)
                    nc.vector.tensor_tensor(y[n][:], bank[6 + n % 2][:], down_scale[:], ALU.mult).then_inc(y_scaled, 1)
                    dve.wait_ge(y_scaled, tile + 1)
                    nc.vector.tensor_tensor(y[n][:], y[n][:], h[:, tile, :], ALU.add).then_inc(y_added, 1)
                    dve.wait_ge(y_added, tile + 1)
                    statistics(NT + tile, n % 2, y[n][:])
                    normalize(NT + tile, n % 2, y[n][:], y[n][:]).then_inc(y_ready, 1)

        @block.gpsimd
        def _(pool):
            nc.gpsimd.memset(minus_half[:], -0.5).then_inc(consts, 1)
            nc.gpsimd.memset(rms_eps[:], RMS_EPS * HD).then_inc(consts_made, 1)
            nc.gpsimd.memset(ident[:], 1.0).then_inc(consts_made, 1)
            pool.wait_ge(consts_made, 2)
            nc.gpsimd.affine_select(ident[:], ident[:], pattern=[[-1, P]], compare_op=ALU.is_equal, fill=0.0,
                                    base=0, channel_multiplier=1).then_inc(consts, 1)

            def lo(dst, src, hi):
                return nc.gpsimd.tensor_tensor(dst, src, f32(hi), ALU.subtract)

            def split_kv(g):
                pool.wait_ge(kvw_hi_ready, g + 1)
                lo(wkv_lo[:].rearrange("p c n -> p (c n)"), stage_kv,
                   wkv_hi[:].rearrange("p c n -> p (c n)")).then_inc(kvw_ready, 1)

            def split_q(g):
                pool.wait_ge(qw_hi_ready, g + 1)
                lo(wq_lo[:].rearrange("p c n -> p (c n)"), stage_q,
                   wq_hi[:].rearrange("p c n -> p (c n)")).then_inc(qw_ready, 1)

            def split_o(g):
                pool.wait_ge(wow_hi_ready, g + 1)
                lo(wo_lo[:].rearrange("p c n -> p (c n)"), stage_q,
                   wo_hi[:].rearrange("p c n -> p (c n)")).then_inc(wow_ready, 1)

            def tile_rstd(tile):
                pool.wait_ge(sq_sum_ready, tile + 1)
                nc.gpsimd.tensor_tensor(sq_mean[:], sq_sum[:], rms_eps[:], ALU.add).then_inc(mean_ready, 1)
                pool.wait_ge(mean_ready, tile + 1)
                nc.gpsimd.tensor_tensor(rstd[:], sq_mean[:], minus_half[:, 0:GROUP + 1], ALU.pow).then_inc(rstd_ready, 1)

            def norm_probs(k, i):
                wait_apart(pool, inv_ready, 2 * k + 1 + i // 2)
                cols = probs[:, COL[i]:COL[i] + WIDTH[i]]
                nc.gpsimd.tensor_scalar(cols, cols, row_inv[:, i:i + 1], 0.0, ALU.mult, ALU.add).then_inc(probs_ready, 1)

            def layer_rstd(tile, s):
                wait_apart(pool, var_ready, tile + 1)
                nc.gpsimd.tensor_scalar(ln_var_eps[:, s, :], ln_mean_var[:, s, 1:2], 1.0, LN_EPS, ALU.mult, ALU.add).then_inc(var_eps_ready, 1)
                pool.wait_ge(var_eps_ready, tile + 1)
                nc.gpsimd.tensor_tensor(ln_rstd[:, s, :], ln_var_eps[:, s, :], minus_half[:, 0:1], ALU.pow).then_inc(ln_rstd_ready, 1)

            def group(g, last):
                for b in range(BATCH):
                    for n in range(GROUP):
                        k = 8 * g + 4 * b + n
                        has_scores = not (last and b == 1 and n == GROUP - 1)
                        if has_tile(last, b, n):
                            tile_rstd(k + LEAD)
                        if has_scores:
                            norm_probs(k + 1, 0)
                            norm_probs(k + 1, 1)
                            norm_probs(k + 1, 2)
                        if b == 1 and not last:
                            wait_apart(pool, biased, 4 * k + 4)
                            nc.gpsimd.tensor_scalar(neg_bias[:, n, :], neg_bias[:, n, :], 0.5, 0.0, ALU.mult, ALU.add).then_inc(bias_ready, 1)
                        if b == 0 and n == 2 and not last:
                            split_kv(g + 1)
                        if b == 0 and n == 3:
                            split_o(g)
                        if last and b == 1:
                            layer_rstd(n, n % 2)

            split_kv(0)
            split_q(0)
            for i in range(GROUP):
                bias = neg_bias[:, i, :]
                nc.gpsimd.iota(bias, [[-1, SEQ]], base=SEQ - P, channel_multiplier=1,
                               allow_small_or_imprecise_dtypes=True).then_inc(consts_made, 1)
                pool.wait_ge(consts_made, 2 * i + 3)
                nc.gpsimd.tensor_scalar(bias, bias, SLOPES[i], None, ALU.mult).then_inc(consts_made, 1)
                pool.wait_ge(consts_made, 2 * i + 4)
                nc.gpsimd.affine_select(bias, bias, pattern=[[-1, SEQ]], compare_op=ALU.is_ge, fill=MASKED,
                                        base=SEQ - P, channel_multiplier=1).then_inc(bias_ready, 1)
            for n in range(TB + 1):
                tile_rstd(n)
            for i in range(3):
                norm_probs(0, i)
            group(0, False)
            with pool.Fori(1, KV_HEADS - 1) as g:
                group(g, False)

            def split_down(pair, s, rows):
                j = 2 * pair + s
                wait_apart(pool, down_in[s], 16 * (pair + 1))
                part = bass.ds(j, 1)
                hi_part = down_hi[0:rows, part, :].rearrange("p j d -> p (j d)")
                lo_part = down_lo[0:rows, part, :].rearrange("p j d -> p (j d)")
                nc.gpsimd.tensor_copy(down_f[s][0:rows, :], down_raw[s][0:rows, :]).then_inc(down_f_ready, 1)
                wait_apart(pool, down_f_ready, j + 1)
                nc.gpsimd.tensor_copy(hi_part, down_f[s][0:rows, :]).then_inc(down_hi_ready, 1)
                pool.wait_ge(down_hi_ready, j + 1)
                lo(lo_part, down_f[s][0:rows, :], hi_part).then_inc(down_ready, 1)

            group(KV_HEADS - 1, True)
            for t in range(TB, NT):
                layer_rstd(t, t % 2)
            with pool.Fori(0, FULL // 2) as pair:
                for s in range(2):
                    split_down(pair, s, P)
            split_down(FULL // 2, 0, REST)
            with pool.Fori(0, NT // 2) as pair:
                for s in range(2):
                    layer_rstd(NT + 2 * pair + s, s)


def kernel(L0_attn_x, L0_attn_Wq, L0_attn_Wk, L0_attn_Wv, L0_attn_Wo, L0_attn_q_norm_w, L0_attn_k_norm_w,
           L0_ffn_gate_w, L0_ffn_gate_s, L0_ffn_up_w, L0_ffn_up_s, L0_ffn_down_w, L0_ffn_down_s):
    import numpy as np
    import concourse.bacc as bacc
    from concourse.bass_utils import run_bass_kernel_spmd

    def chunked(w, groups):
        w = np.asarray(w).reshape(groups, -1, NC, P)
        return np.ascontiguousarray(w.transpose(0, 3, 2, 1)).reshape(groups, P, -1)

    def hidden_rows(gate, up):
        both = np.stack([gate, up]).reshape(2, -1, min(P, gate.shape[0]), NC, P)
        return np.ascontiguousarray(both.transpose(1, 4, 0, 3, 2)).reshape(both.shape[1], P, -1)

    x = np.asarray(L0_attn_x).reshape(TOK, DM)
    wk = np.asarray(L0_attn_Wk).reshape(KV_HEADS, HD, DM)
    wv = np.asarray(L0_attn_Wv).reshape(KV_HEADS, HD, DM)
    wo = np.asarray(L0_attn_Wo).reshape(DM, KV_HEADS, GROUP, HD)
    gate, up, down = (np.asarray(a) for a in (L0_ffn_gate_w, L0_ffn_up_w, L0_ffn_down_w))
    gate_s, up_s = np.asarray(L0_ffn_gate_s), np.asarray(L0_ffn_up_s)
    arrays = {
        "xT": np.ascontiguousarray(x.reshape(TOK, NC, P).transpose(2, 1, 0)).reshape(P, NC * TOK),
        "x": x,
        "wq": chunked(L0_attn_Wq, KV_HEADS),
        "wkv": chunked(np.concatenate([wk, wv], axis=1), KV_HEADS),
        "wo": np.ascontiguousarray(wo.transpose(1, 3, 2, 0)).reshape(KV_HEADS, HD, GROUP * DM),
        "q_norm": np.asarray(L0_attn_q_norm_w).reshape(HD, 1),
        "k_norm": np.asarray(L0_attn_k_norm_w).reshape(HD, 1),
        "gate_up": hidden_rows(gate[:FULL * P], up[:FULL * P]),
        "gate_up_rest": hidden_rows(gate[FULL * P:], up[FULL * P:])[0],
        "down": np.ascontiguousarray(down[:, :FULL * P].T).reshape(FULL, P, DM),
        "down_rest": np.ascontiguousarray(down[:, FULL * P:].T),
        "gate_s": np.ascontiguousarray(gate_s[:FULL * P].reshape(FULL, P).T),
        "gate_s_rest": gate_s[FULL * P:].reshape(REST, 1),
        "up_s": np.ascontiguousarray(up_s[:FULL * P].reshape(FULL, P).T),
        "up_s_rest": up_s[FULL * P:].reshape(REST, 1),
        "down_s": np.asarray(L0_ffn_down_s),
    }
    arrays = {name: np.ascontiguousarray(a) for name, a in arrays.items()}
    nc = bacc.Bacc("TRN2", target_bir_lowering=False, num_devices=1)
    ins = [nc.dram_tensor(name, a.shape, mybir.dt.from_np(a.dtype), kind="ExternalInput").ap() for name, a in arrays.items()]
    out = nc.dram_tensor("out", (NT, P, DM), F32, kind="ExternalOutput").ap()
    block_kernel(nc, *ins, out)
    result = run_bass_kernel_spmd(nc, [arrays], core_ids=[0])
    return result.results[0]["out"].reshape(BATCH, SEQ, DM)
```

```python
import math
from contextlib import ExitStack

import concourse.bass as bass
from concourse import mybir

F32 = mybir.dt.float32
F32R = mybir.dt.float32r
I32 = mybir.dt.int32
ALU = mybir.AluOpType
ACT = mybir.ActivationFunctionType
AX_X = mybir.AxisListType.X

P = 128
BATCH, SEQ, DM = 2, 512, 512
TOK = BATCH * SEQ
HEADS, KV_HEADS, HD = 32, 8, 128
GROUP = HEADS // KV_HEADS
DFF = 1376
NT = TOK // P
TB = SEQ // P
NC = DM // P
QW = GROUP * HD
KVW = 2 * HD
TILES = KV_HEADS * NT
FULL = DFF // P
REST = DFF - FULL * P
NF = FULL + 1
RMS_EPS, LN_EPS = 1e-6, 1e-5
SCALE = HD / math.sqrt(HD)
SLOPE0 = 2 ** (-2 ** (-(math.log2(HEADS) - 3)))
SLOPES = [SLOPE0 * SLOPE0 ** i for i in range(GROUP)]
MASKED = 1e30 * 2 ** KV_HEADS
HUGE = 3.0e38
STEPS = KV_HEADS * BATCH * GROUP
SCAN = 3 * DFF * DM // (P * STEPS)
NARROW = 2.0 ** 12

WIDTH = [P * (i + 1) for i in range(TB)]
COL = [sum(WIDTH[:i]) for i in range(TB)]
SCORES = sum(WIDTH)
BANKS = [[0], [1, 3], [2]]
PT_COL = {0: 0, 1: SEQ, 3: SEQ + 384, 2: 2 * SEQ}
PT_WIDTH = {j: SEQ - P * j for j in range(TB)}
BANK_COL = [0, SEQ, 2 * SEQ]
BANK_WIDTH = [sum(PT_WIDTH[j] for j in bank) for bank in BANKS]


def block_kernel(nc, xT, x, wq, wkv, wo, q_norm, k_norm, gate_up, gate_up_rest, down, down_rest,
                 gate_s, gate_s_rest, up_s, up_s_rest, down_s, ffn_weights, out):
    ctx = ExitStack()
    with ctx:
        def sem(name):
            return ctx.enter_context(nc.semaphore(name))

        def tensor(stack, name, shape, dt=F32):
            return stack.enter_context(nc.sbuf_tensor(name, shape, dt))

        h = tensor(ctx, "h", [P, NT, DM])
        ident = tensor(ctx, "ident", [P, P])
        rms_eps = tensor(ctx, "rms_eps", [P, GROUP + 1])
        minus_half = tensor(ctx, "minus_half", [P, 8])
        ln_stats = tensor(ctx, "ln_stats", [P, 2, 6])
        ln_mean_var = tensor(ctx, "ln_mean_var", [P, 2, 2])
        ln_var_eps = tensor(ctx, "ln_var_eps", [P, 2, 1])
        ln_rstd = tensor(ctx, "ln_rstd", [P, 2, 1])
        scan_raw = tensor(ctx, "scan_raw", [P, SCAN], I32)
        scan_max = tensor(ctx, "scan_max", [P, STEPS])
        row_max = tensor(ctx, "row_max", [P, 1])
        weight_max = tensor(ctx, "weight_max", [1, 1])
        narrow = tensor(ctx, "narrow", [1, 1], I32)

        attn = ExitStack()
        stage = tensor(attn, "stage", [P, NC * (KVW + QW)])
        stage_kv, stage_q = stage[:, 0:NC * KVW], stage[:, NC * KVW:]
        wkv_hi = tensor(attn, "wkv_hi", [P, NC, KVW], F32R)
        wkv_lo = tensor(attn, "wkv_lo", [P, NC, KVW], F32R)
        wq_hi = tensor(attn, "wq_hi", [P, NC, QW], F32R)
        wq_lo = tensor(attn, "wq_lo", [P, NC, QW], F32R)
        xT_hi = tensor(attn, "xT_hi", [P, NC, TOK], F32R)
        xT_lo = tensor(attn, "xT_lo", [P, NC, TOK], F32R)
        wo_hi = tensor(attn, "wo_hi", [P, GROUP, DM], F32R)
        wo_lo = tensor(attn, "wo_lo", [P, GROUP, DM], F32R)
        qT_hi = tensor(attn, "qT_hi", [P, BATCH, GROUP, SEQ], F32R)
        qT_lo = tensor(attn, "qT_lo", [P, BATCH, GROUP, SEQ], F32R)
        kT_hi = tensor(attn, "kT_hi", [P, BATCH, SEQ], F32R)
        kT_lo = tensor(attn, "kT_lo", [P, BATCH, SEQ], F32R)
        v_hi = tensor(attn, "v_hi", [P, BATCH, TB, HD], F32R)
        v_lo = tensor(attn, "v_lo", [P, BATCH, TB, HD], F32R)
        oT_hi = tensor(attn, "oT_hi", [P, BATCH, GROUP, SEQ], F32R)
        oT_lo = tensor(attn, "oT_lo", [P, BATCH, GROUP, SEQ], F32R)
        probs = tensor(attn, "probs", [P, SCORES])
        pT_hi = tensor(attn, "pT_hi", [P, SCORES], F32R)
        pT_lo = tensor(attn, "pT_lo", [P, SCORES], F32R)
        neg_bias = tensor(attn, "neg_bias", [P, GROUP, SEQ])
        qk = tensor(attn, "qk", [P, GROUP + 1, HD])
        neg_max = tensor(attn, "neg_max", [P, TB])
        row_sum = tensor(attn, "row_sum", [P, TB])
        row_inv = tensor(attn, "row_inv", [P, TB])
        sq_sum = tensor(attn, "sq_sum", [P, GROUP + 1])
        sq_mean = tensor(attn, "sq_mean", [P, GROUP + 1])
        rstd = tensor(attn, "rstd", [P, GROUP + 1])
        norm_w = tensor(attn, "norm_w", [P, 2])
        k_scale = tensor(attn, "k_scale", [P, 1])
        attn.close()

        ffn = ExitStack()
        gu_raw = [tensor(ffn, f"gu_raw{s}", [P, 2, NC, P], I32) for s in range(2)]
        gu_rest_raw = tensor(ffn, "gu_rest_raw", [P, 2, NC, REST], I32)
        gate_scale = tensor(ffn, "gate_scale", [P, NF])
        up_scale = tensor(ffn, "up_scale", [P, NF])
        down_scale = tensor(ffn, "down_scale", [P, DM])
        gu_hi = [tensor(ffn, f"gu_hi{s}", [P, 2, NC, P], F32R) for s in range(2)]
        gu_lo = [tensor(ffn, f"gu_lo{s}", [P, 2, NC, P], F32R) for s in range(2)]
        gu_rest_hi = tensor(ffn, "gu_rest_hi", [P, 2, NC, REST], F32R)
        gu_rest_lo = tensor(ffn, "gu_rest_lo", [P, 2, NC, REST], F32R)
        hT_hi = tensor(ffn, "hT_hi", [P, NC, TOK], F32R)
        hT_lo = tensor(ffn, "hT_lo", [P, NC, TOK], F32R)
        act_hi = tensor(ffn, "act_hi", [P, NF, SEQ], F32R)
        act_lo = tensor(ffn, "act_lo", [P, NF, SEQ], F32R)
        down_raw = tensor(ffn, "down_raw", [P, NF, DM], I32)
        down_hi = tensor(ffn, "down_hi", [P, NF, DM], F32R)
        down_lo = tensor(ffn, "down_lo", [P, NF, DM], F32R)
        silu = [tensor(ffn, f"silu{s}", [P, SEQ]) for s in range(2)]
        gated = [tensor(ffn, f"gated{s}", [P, SEQ]) for s in range(2)]
        y = [down_raw[:, n, :].bitcast(F32) for n in range(TB)]
        ffn.close()

        bank = [ctx.enter_context(nc.psum_tensor(f"bank{i}", [P, 512], F32)) for i in range(8)]
        score_bank = bank[0:2]
        q_bank, kv_bank, o_bank, wo_bank = bank[2], bank[3], bank[6], bank[7]
        tr_bank = bank[4:6]
        tail_bank = [wo_bank, o_bank]
        h_bank = [bank[i] for i in (4, 5, 1, 3, 4, 5, 6, 7)]

        x_in, kv_in, q_in, wo_in, norm_in = (sem(f"{n}_in") for n in ("x", "kv", "q", "wo", "norm"))
        xT_in = [sem(f"xT_in{b}") for b in range(BATCH)]
        rest_in, scales_in, y_out = (sem(n) for n in ("rest_in", "scales_in", "y_out"))
        gu_in = [sem(f"gu_in{s}") for s in range(2)]
        down_in = [sem(f"down_in{pair}") for pair in range(FULL // 2 + 1)]
        consts_made = sem("consts_made")
        apart = sem("apart")
        consts, bias_ready, k_scale_ready = sem("consts"), sem("bias_ready"), sem("k_scale_ready")
        xT_hi_ready, xT_ready = sem("xT_hi_ready"), sem("xT_ready")
        kvw_hi_ready, kvw_ready = sem("kvw_hi_ready"), sem("kvw_ready")
        qw_hi_ready, qw_ready = sem("qw_hi_ready"), sem("qw_ready")
        wow_hi_ready, wow_ready = sem("wow_hi_ready"), sem("wow_ready")
        kv_done, q_done, v_hi_ready, v_ready = sem("kv_done"), sem("q_done"), sem("v_hi_ready"), sem("v_ready")
        sq_ready, sq_sum_ready, mean_ready, rstd_ready = sem("sq_ready"), sem("sq_sum_ready"), sem("mean_ready"), sem("rstd_ready")
        normed, qT_done, kT_done = sem("normed"), sem("qT_done"), sem("kT_done")
        qT_hi_ready, kT_hi_ready, qT_ready, kT_ready = sem("qT_hi_ready"), sem("kT_hi_ready"), sem("qT_ready"), sem("kT_ready")
        scores_done, biased, exp_done, inv_ready, probs_ready, probs3_ready = (
            sem(n) for n in ("scores_done", "biased", "exp_done", "inv_ready", "probs_ready", "probs3_ready"))
        pT_done, pT_hi_ready, pT_ready = sem("pT_done"), sem("pT_hi_ready"), sem("pT_ready")
        o_done, oT_hi_ready, oT_ready = sem("o_done"), sem("oT_hi_ready"), sem("oT_ready")
        wo_done, added = sem("wo_done"), sem("added")
        stats_ready, var_ready, var_eps_ready, ln_rstd_ready, ln_done = (
            sem(n) for n in ("stats_ready", "var_ready", "var_eps_ready", "ln_rstd_ready", "ln_done"))
        hT_done, hT_hi_ready, hT_ready = sem("hT_done"), sem("hT_hi_ready"), sem("hT_ready")
        scan_in, scanned, row_max_ready, row_max_done, weight_max_ready, narrow_ready = (
            sem(n) for n in ("scan_in", "scanned", "row_max_ready", "row_max_done", "weight_max_ready", "narrow_ready"))
        gu_hi_ready, gu_ready, rest_hi_ready, rest_ready = (
            sem(n) for n in ("gu_hi_ready", "gu_ready", "rest_hi_ready", "rest_ready"))
        down_hi_ready, down_ready = sem("down_hi_ready"), sem("down_ready")
        gate_done, up_done, silu_ready, gated_ready = sem("gate_done"), sem("up_done"), sem("silu_ready"), sem("gated_ready")
        act_hi_ready, act_ready = sem("act_hi_ready"), sem("act_ready")
        y_done, y_scaled, y_added, y_ready = sem("y_done"), sem("y_scaled"), sem("y_added"), sem("y_ready")

        def wait(engine, semaphore, value):
            if not isinstance(value, int) or value > 0:
                engine.wait_ge(semaphore, value)

        def wait_apart(engine, semaphore, value):
            engine.wait_ge(semaphore, value)
            engine.sem_inc(apart, 1)

        def f32(ap):
            return ap.bitcast(F32)

        block = ctx.enter_context(nc.Block())

        @block.sync
        def _(sp):
            raw, src = (a.rearrange("p (c b q) -> p c b q", c=NC, b=BATCH) for a in (h[:].rearrange("p t d -> p (t d)"), xT))
            sp.dma_start(raw[:, :, 0, :], src[:, :, 0, :]).then_inc(xT_in[0], 16)
            sp.dma_start(stage_kv, wkv[0, :, :]).then_inc(kv_in, 16)
            sp.dma_start(stage_q, wq[0, :, :]).then_inc(q_in, 16)
            sp.dma_start(norm_w[:, 0:1], q_norm).then_inc(norm_in, 16)
            sp.dma_start(norm_w[:, 1:2], k_norm).then_inc(norm_in, 16)
            sp.dma_start(raw[:, :, 1, :], src[:, :, 1, :]).then_inc(xT_in[1], 16)
            sp.wait_ge(xT_ready, BATCH * NC)
            sp.dma_start(h[:], x.rearrange("(t p) d -> p t d", p=P)).then_inc(x_in, 16)
            sp.wait_ge(kvw_ready, 1)
            sp.dma_start(stage_kv, wkv[1, :, :]).then_inc(kv_in, 16)
            sp.wait_ge(qw_ready, 1)
            sp.dma_start(stage_q, wq[1, :, :]).then_inc(q_in, 16)
            sp.dma_start(scan_raw[:], ffn_weights[0, :, :]).then_inc(scan_in, 16)

            def load_scan(step):
                sp.wait_ge(scanned, step + 1)
                sp.dma_start(scan_raw[:], ffn_weights[bass.ds(step + 1, 1), :, :].rearrange("s p n -> (s p) n")).then_inc(scan_in, 16)

            def load_group(g, kv, q):
                for n in range(2):
                    load_scan(8 * g + n)
                sp.wait_ge(qw_ready, g + 2)
                sp.dma_start(stage_q, wo[bass.ds(g, 1), :, :].rearrange("g p n -> (g p) n")).then_inc(wo_in, 16)
                if kv:
                    sp.wait_ge(kvw_ready, g + 2)
                    sp.dma_start(stage_kv, wkv[bass.ds(g + 2, 1), :, :].rearrange("g p n -> (g p) n")).then_inc(kv_in, 16)
                for n in range(2, 4):
                    load_scan(8 * g + n)
                sp.wait_ge(wow_ready, g + 1)
                sp.dma_start(stage_q, q[bass.ds(g + 2 if kv else g + 1, 1), :, :].rearrange("g p n -> (g p) n")).then_inc(q_in if kv else wo_in, 16)
                for n in range(4, 8):
                    load_scan(8 * g + n)

            with sp.Fori(0, KV_HEADS - 2) as g:
                load_group(g, True, wq)
            load_group(KV_HEADS - 2, False, wo)
            for n in range(4):
                load_scan(STEPS - 8 + n)
            sp.wait_ge(wow_ready, KV_HEADS)
            sp.wait_ge(q_done, TILES)
            sp.dma_start(gu_rest_raw[:].rearrange("p a c f -> p (a c f)"), gate_up_rest).then_inc(rest_in, 16)

            def load_pair(b, pair):
                for s in range(2):
                    wait(sp, gu_ready, FULL * b + 2 * pair + s - 1)
                    sp.dma_start(gu_raw[s][:].rearrange("p a c f -> p (a c f)"),
                                 gate_up[bass.ds(2 * pair + s, 1), :, :].rearrange("j p n -> (j p) n")).then_inc(gu_in[s], 16)

            load_pair(0, 0)
            sp.dma_start(gate_scale[:, 0:FULL], gate_s).then_inc(scales_in, 16)
            sp.dma_start(gate_scale[0:REST, FULL:NF], gate_s_rest).then_inc(scales_in, 16)
            sp.dma_start(up_scale[:, 0:FULL], up_s).then_inc(scales_in, 16)
            sp.dma_start(up_scale[0:REST, FULL:NF], up_s_rest).then_inc(scales_in, 16)
            sp.dma_start(down_scale[:], down_s.partition_broadcast(P)).then_inc(scales_in, 16)
            for n in range(4, 7):
                load_scan(STEPS - 8 + n)
            sp.wait_ge(added, TILES)
            for pair in range(1, FULL // 2 + 1):
                if pair < FULL // 2:
                    load_pair(0, pair)
                sp.dma_start(down_raw[:, 2 * pair - 2:2 * pair, :],
                             down[2 * pair - 2:2 * pair, :, :].rearrange("j p d -> p j d")).then_inc(down_in[pair - 1], 16)
            sp.dma_start(down_raw[0:REST, FULL, :], down_rest).then_inc(down_in[FULL // 2], 16)
            load_pair(1, 0)
            with sp.Fori(1, FULL // 2) as pair:
                load_pair(1, pair)
            for t in range(NT):
                sp.wait_ge(y_ready, t + 1)
                sp.dma_start(out[t, :, :], y[t % TB]).then_inc(y_out, 16)
            sp.wait_ge(y_out, 16 * NT)

        LEAD = 5

        def has_tile(last, b, n):
            return not last or 4 * b + n + LEAD < NT

        def tile_row(b, n):
            return 1 - b if n < 3 else b

        @block.tensor
        def _(pe):
            def product(dst, a_hi, a_lo, b_hi, b_lo, first, last):
                nc.tensor.matmul(dst, a_hi, b_lo, start=first, stop=False)
                nc.tensor.matmul(dst, a_lo, b_hi, start=False, stop=False)
                return nc.tensor.matmul(dst, a_hi, b_hi, start=False, stop=last)

            def project_kv(dst, b, n):
                t = slice((TB * b + n) * P, (TB * b + n + 1) * P)
                for c in range(NC):
                    last = product(dst[:, 0:KVW], xT_hi[:, c, t], xT_lo[:, c, t],
                                   wkv_hi[:, c, :], wkv_lo[:, c, :], c == 0, c == NC - 1)
                last.then_inc(kv_done, 1)

            def project_q(dst, b, n):
                t = slice((TB * b + n) * P, (TB * b + n + 1) * P)
                for c in range(NC):
                    last = product(dst[:], xT_hi[:, c, t], xT_lo[:, c, t],
                                   wq_hi[:, c, :], wq_lo[:, c, :], c == 0, c == NC - 1)
                last.then_inc(q_done, 1)

            def transpose_qk(tile, k_bank):
                pe.wait_ge(normed, tile + 1)
                for i in range(GROUP):
                    last = nc.tensor.transpose(tr_bank[1][:, i * P:(i + 1) * P], qk[:, i, :], ident[:])
                last.then_inc(qT_done, 1)
                pe.wait_ge(v_ready, tile + 1)
                nc.tensor.transpose(k_bank[:, KVW:KVW + P], qk[:, GROUP, :], ident[:]).then_inc(kT_done, 1)

            def scores(k, b, n, i):
                wait(pe, biased, 4 * k + i - 1)
                q = slice(i * P, (i + 1) * P)
                product(score_bank[i % 2][:, 0:WIDTH[i]], qT_hi[:, b, n, q], qT_lo[:, b, n, q],
                        kT_hi[:, b, 0:WIDTH[i]], kT_lo[:, b, 0:WIDTH[i]], True, True).then_inc(scores_done, 1)

            def transpose_probs(which):
                for j in BANKS[which]:
                    for i in range(j, TB):
                        col = PT_COL[j] - BANK_COL[which] + (i - j) * P
                        last = nc.tensor.transpose(tr_bank[which % 2][:, col:col + P],
                                                   probs[:, COL[i] + j * P:COL[i] + (j + 1) * P], ident[:])
                last.then_inc(pT_done, 1)

            def attend(b, j):
                cols = slice(PT_COL[j], PT_COL[j] + PT_WIDTH[j])
                return product(o_bank[:, j * P:SEQ], v_hi[:, b, j, :], v_lo[:, b, j, :],
                               pT_hi[:, cols], pT_lo[:, cols], j == 0, j == 2)

            def project_out(b, n, half, dst):
                q = slice(n * P, (n + 1) * P)
                for i in (2 * half, 2 * half + 1):
                    last = product(dst[:], oT_hi[:, b, i, q], oT_lo[:, b, i, q],
                                   wo_hi[:, i, :], wo_lo[:, i, :], i == 0, i == GROUP - 1)
                if half == 1:
                    last.then_inc(wo_done, 1)

            def group(g, first, last):
                for b in range(BATCH):
                    for n in range(GROUP):
                        k = 8 * g + 4 * b + n
                        has_next = has_tile(last, b, n)
                        has_prev = not (first and b == 0)
                        has_scores = not (last and b == 1 and n == GROUP - 1)
                        pe.wait_ge(probs_ready, 3 * k + 3)
                        pe.wait_ge(probs3_ready, k + 1)
                        wait(pe, pT_ready, 3 * k)
                        transpose_probs(0)
                        pe.wait_ge(qT_ready, k + LEAD if has_tile(last, b, n - 1) or n == 0 and b == 0 else TILES)
                        transpose_probs(1)
                        if has_next:
                            if b == 0 and n == 3:
                                pe.wait_ge(kvw_ready, g + 2)
                            pe.wait_ge(kT_ready, k + LEAD)
                            project_kv(kv_bank, tile_row(b, n), (n + 1) % TB)
                            if b == 0 and n == 3:
                                pe.wait_ge(qw_ready, g + 2)
                            pe.wait_ge(normed, k + LEAD)
                            project_q(q_bank, tile_row(b, n), (n + 1) % TB)
                        pe.wait_ge(pT_ready, 3 * k + 1)
                        transpose_probs(2)
                        if has_scores:
                            sb, sn = (b, n + 1) if n < 3 else (1 - b, 0)
                            if n == 3:
                                pe.wait_ge(qT_ready, 8 * g + 4 * b + 8)
                                pe.wait_ge(kT_ready, 8 * g + 4 * b + 8)
                            scores(k + 1, sb, sn, 0)
                            scores(k + 1, sb, sn, 1)
                        wait(pe, oT_ready, k)
                        attend(b, 0)
                        pe.wait_ge(pT_ready, 3 * k + 2)
                        attend(b, 1)
                        attend(b, 3)
                        if has_scores:
                            scores(k + 1, sb, sn, 2)
                            scores(k + 1, sb, sn, 3)
                        pe.wait_ge(pT_ready, 3 * k + 3)
                        attend(b, 2).then_inc(o_done, 1)
                        if has_prev:
                            if n == 0:
                                pe.wait_ge(oT_ready, 8 * g + 4 * b)
                                if b == 1:
                                    pe.wait_ge(wow_ready, g + 1)
                            wait(pe, added, k - 4)
                            project_out(1 - b, n, 0, wo_bank)
                        if has_next:
                            transpose_qk(k + LEAD, kv_bank)
                        if has_prev:
                            project_out(1 - b, n, 1, wo_bank)

            first_q = [q_bank, score_bank[0], score_bank[1], o_bank]
            first_kv = [kv_bank, wo_bank, tr_bank[0], kv_bank]
            pe.wait_ge(consts, 2)
            pe.wait_ge(xT_ready, NC)
            pe.wait_ge(kvw_ready, 1)
            for n in range(TB):
                if n == 3:
                    pe.wait_ge(kT_ready, 1)
                project_kv(first_kv[n], 0, n)
                if n == 0:
                    pe.wait_ge(qw_ready, 1)
                project_q(first_q[n], 0, n)
                if n > 0:
                    wait(pe, qT_ready, n - 1)
                    transpose_qk(n - 1, first_kv[n - 1])
            pe.wait_ge(qT_ready, 3)
            transpose_qk(3, first_kv[3])
            pe.wait_ge(xT_ready, BATCH * NC)
            pe.wait_ge(kT_ready, TB)
            project_kv(kv_bank, 1, 0)
            pe.wait_ge(qT_ready, TB)
            scores(0, 0, 0, 0)
            scores(0, 0, 0, 1)
            project_q(q_bank, 1, 0)
            scores(0, 0, 0, 2)
            scores(0, 0, 0, 3)
            transpose_qk(4, kv_bank)
            group(0, True, False)
            with pe.Fori(1, KV_HEADS - 1) as g:
                group(g, False, False)
            group(KV_HEADS - 1, False, True)

            def transpose_h(t):
                pe.wait_ge(ln_done, t + 1)
                for c in range(NC):
                    last = nc.tensor.transpose(h_bank[t][:, c * P:(c + 1) * P], h[:, t, c * P:(c + 1) * P], ident[:])
                last.then_inc(hT_done, 1)

            pe.wait_ge(oT_ready, STEPS)
            for n in range(GROUP):
                pe.wait_ge(added, TILES - 4 if n == 0 else TILES - 4 + n - 1)
                project_out(1, n, 0, tail_bank[n % 2])
                project_out(1, n, 1, tail_bank[n % 2])
                if n == 0:
                    for t in range(TB - 1):
                        transpose_h(t)
                    pe.wait_ge(row_max_ready, 1)
                    nc.tensor.transpose(score_bank[0][0:1, 0:P], row_max[:], ident[:]).then_inc(row_max_done, 1)
                if n == 1:
                    transpose_h(TB - 1)

            def feed_forward(has_lo):
                def hidden(b, banks, weights_hi, weights_lo, rows):
                    tok = slice(SEQ * b, SEQ * (b + 1))
                    for a, done in ((0, gate_done), (1, up_done)):
                        dst = banks[a][0:rows, :]
                        for c in range(NC):
                            nc.tensor.matmul(dst, weights_hi[:, a, c, :], hT_lo[:, c, tok], start=c == 0, stop=False)
                            if has_lo:
                                nc.tensor.matmul(dst, weights_lo[:, a, c, :], hT_hi[:, c, tok], start=False, stop=False)
                            last = nc.tensor.matmul(dst, weights_hi[:, a, c, :], hT_hi[:, c, tok], start=False, stop=c == NC - 1)
                        last.then_inc(done, 1)

                def hidden_pair(b, pair):
                    for s in range(2):
                        pe.wait_ge(gu_ready, FULL * b + 2 * pair + s + 1)
                        wait(pe, gated_ready, NF * b + 2 * pair + s - 1)
                        hidden(b, (bank[s], bank[2 + s]), gu_hi[s], gu_lo[s], P)

                def down_tile(b, n):
                    dst = bank[6 + n % 2][:]
                    for j in range(NF):
                        rows = P if j < FULL else REST
                        q = slice(n * P, (n + 1) * P)
                        nc.tensor.matmul(dst, act_lo[0:rows, j, q], down_hi[0:rows, j, :], start=j == 0, stop=False)
                        if has_lo:
                            nc.tensor.matmul(dst, act_hi[0:rows, j, q], down_lo[0:rows, j, :], start=False, stop=False)
                        last = nc.tensor.matmul(dst, act_hi[0:rows, j, q], down_hi[0:rows, j, :], start=False, stop=j == NF - 1)
                    last.then_inc(y_done, 1)

                for b in range(BATCH):
                    pe.wait_ge(hT_ready, TB * b + TB)
                    hidden_pair(b, 0)
                    if b == 0:
                        pe.wait_ge(added, TILES)
                        for t in range(TB, NT):
                            transpose_h(t)
                    with pe.Fori(1, FULL // 2) as pair:
                        hidden_pair(b, pair)
                    pe.wait_ge(rest_ready, 1)
                    if b == 0:
                        pe.wait_ge(hT_ready, NT)
                    else:
                        pe.wait_ge(y_scaled, TB)
                    hidden(b, bank[6:8], gu_rest_hi, gu_rest_lo, REST)
                    for n in range(TB):
                        if n < 2:
                            pe.wait_ge(act_ready, NF * b + NF)
                        else:
                            pe.wait_ge(y_scaled, TB * b + n - 1)
                        if b == 0 and n == 0:
                            pe.wait_ge(down_ready, FULL // 2 + 1)
                        down_tile(b, n)

            pe.wait_ge(narrow_ready, 1)
            is_narrow = pe.value_load(narrow[0:1, 0:1], min_val=0, max_val=1)
            with pe.If(is_narrow == 0):
                feed_forward(True)
            with pe.If(is_narrow == 1):
                feed_forward(False)

        @block.scalar
        def _(act):
            def hi(dst, src):
                return nc.scalar.activation(dst, src, ACT.Copy)

            def split_kv(g):
                wait(act, kv_done, 8 * g)
                act.wait_ge(kv_in, 16 * g + 16)
                hi(wkv_hi[:].rearrange("p c n -> p (c n)"), stage_kv).then_inc(kvw_hi_ready, 1)

            def split_q(g):
                wait(act, q_done, 8 * g)
                act.wait_ge(q_in, 16 * g + 16)
                hi(wq_hi[:].rearrange("p c n -> p (c n)"), stage_q).then_inc(qw_hi_ready, 1)

            def split_o(g):
                wait(act, wo_done, 8 * g)
                act.wait_ge(wo_in, 16 * g + 16)
                hi(wo_hi[:].rearrange("p c n -> p (c n)"), stage_q).then_inc(wow_hi_ready, 1)

            def tile_squares(tile, from_q, from_kv):
                wait(act, kT_done, tile)
                act.wait_ge(kv_done, tile + 1)
                nc.scalar.activation(qk[:, GROUP, :], from_kv[:, 0:HD], ACT.Square)
                act.wait_ge(q_done, tile + 1)
                nc.scalar.activation(qk[:, 0:GROUP, :].rearrange("p i d -> p (i d)"), from_q[:], ACT.Square).then_inc(sq_ready, 1)

            def tile_v(b, n, from_kv):
                hi(v_hi[:, b, n, :], from_kv[:, HD:KVW]).then_inc(v_hi_ready, 1)

            def tile_qkT(tile, b, n, from_k):
                act.wait_ge(qT_done, tile + 1)
                hi(qT_hi[:, b, :, n * P:(n + 1) * P], tr_bank[1][:].rearrange("p (i q) -> p i q", i=GROUP)).then_inc(qT_hi_ready, 1)
                act.wait_ge(kT_done, tile + 1)
                nc.scalar.activation(kT_hi[:, b, n * P:(n + 1) * P], from_k[:, KVW:KVW + P], ACT.Copy,
                                     scale=k_scale[:, 0:1]).then_inc(kT_hi_ready, 1)

            def exponentials(k, i):
                act.wait_ge(biased, 4 * k + i + 1)
                cols = probs[:, COL[i]:COL[i] + WIDTH[i]]
                nc.scalar.activation(cols, cols, ACT.Exp, bias=neg_max[:, i:i + 1], scale=-1.0,
                                     accum_out=row_sum[:, i:i + 1]).then_inc(exp_done, 1)

            def split_pT(k, which):
                act.wait_ge(pT_done, 3 * k + which + 1)
                hi(pT_hi[:, BANK_COL[which]:BANK_COL[which] + BANK_WIDTH[which]],
                   tr_bank[which % 2][:, 0:BANK_WIDTH[which]]).then_inc(pT_hi_ready, 1)

            def group(g, first, last):
                for b in range(BATCH):
                    for n in range(GROUP):
                        k = 8 * g + 4 * b + n
                        has_next = has_tile(last, b, n)
                        has_scores = not (last and b == 1 and n == GROUP - 1)
                        wait(act, o_done, k)
                        split_pT(k, 0)
                        split_pT(k, 1)
                        if has_next:
                            tile_squares(k + LEAD, q_bank, kv_bank)
                        split_pT(k, 2)
                        if has_next and n < 3:
                            tile_v(tile_row(b, n), (n + 1) % TB, kv_bank)
                        if has_scores:
                            for i in range(3):
                                exponentials(k + 1, i)
                        act.wait_ge(o_done, k + 1)
                        if has_next and n == 3:
                            tile_v(tile_row(b, n), (n + 1) % TB, kv_bank)
                        hi(oT_hi[:, b, n, :], o_bank[:]).then_inc(oT_hi_ready, 1)
                        if has_scores:
                            exponentials(k + 1, 3)
                        if b == 0 and n == 2 and not last:
                            split_kv(g + 1)
                        if has_next:
                            tile_qkT(k + LEAD, tile_row(b, n), (n + 1) % TB, kv_bank)
                        if b == 0 and n == 2 and not last:
                            split_q(g + 1)
                        if b == 0 and n == 3:
                            split_o(g)

            first_q = [q_bank, score_bank[0], score_bank[1], o_bank, q_bank]
            first_kv = [kv_bank, wo_bank, tr_bank[0], kv_bank, kv_bank]
            raw = h[:].rearrange("p t d -> p (t d)").rearrange("p (c b q) -> p c b q", c=NC, b=BATCH)
            act.wait_ge(xT_in[0], 16)
            for c in range(NC):
                hi(xT_hi[:, c, 0:SEQ], raw[:, c, 0, :]).then_inc(xT_hi_ready, 1)
            split_kv(0)
            split_q(0)
            act.wait_ge(xT_in[1], 16)
            for c in range(NC):
                hi(xT_hi[:, c, SEQ:TOK], raw[:, c, 1, :]).then_inc(xT_hi_ready, 1)
            act.wait_ge(k_scale_ready, 1)
            for n in range(TB):
                tile_squares(n, first_q[n], first_kv[n])
                tile_v(0, n, first_kv[n])
                tile_qkT(n, 0, n, first_kv[n])
            exponentials(0, 0)
            exponentials(0, 1)
            tile_squares(TB, q_bank, kv_bank)
            tile_v(1, 0, kv_bank)
            exponentials(0, 2)
            exponentials(0, 3)
            tile_qkT(TB, 1, 0, kv_bank)
            group(0, True, False)
            with act.Fori(1, KV_HEADS - 1) as g:
                group(g, False, False)
            group(KV_HEADS - 1, False, True)

            def split_gu(b, pair, s):
                act.wait_ge(gu_in[s], 16 * (FULL // 2 * b + pair + 1))
                if b == 0:
                    wait(act, up_done, 2 * pair + s - 1)
                else:
                    act.wait_ge(up_done, FULL + s - 1 if isinstance(pair, int) and pair == 0 else NF + 2 * pair + s - 1)
                hi(gu_hi[s][:], gu_raw[s][:]).then_inc(gu_hi_ready, 1)

            def split_down(pair, rows, chunks):
                act.wait_ge(down_in[pair], 16)
                part = slice(2 * pair, 2 * pair + chunks)
                hi(down_hi[0:rows, part, :], down_raw[0:rows, part, :]).then_inc(down_hi_ready, 1)

            def split_h(t):
                act.wait_ge(hT_done, t + 1)
                hi(hT_hi[:, :, t * P:(t + 1) * P], h_bank[t][:].rearrange("p (c q) -> p c q", c=NC)).then_inc(hT_hi_ready, 1)

            def gate(b, j, s, gate_bank, rows):
                act.wait_ge(gate_done, NF * b + j + 1)
                nc.scalar.activation(silu[s][0:rows, :], gate_bank[0:rows, :], ACT.Silu,
                                     scale=gate_scale[0:rows, bass.ds(j, 1)]).then_inc(silu_ready, 1)

            def split_act(b, j, s, rows):
                act.wait_ge(gated_ready, NF * b + j + 1)
                hi(act_hi[0:rows, bass.ds(j, 1), :].rearrange("p j q -> p (j q)"), gated[s][0:rows, :]).then_inc(act_hi_ready, 1)

            def hidden_pair(b, pair, next_pair):
                for s in range(2):
                    gate(b, 2 * pair + s, s, bank[s], P)
                    if next_pair is not None:
                        split_gu(*next_pair, s)
                    split_act(b, 2 * pair + s, s, P)

            for s in range(2):
                split_gu(0, 0, s)
            act.wait_ge(rest_in, 16)
            hi(gu_rest_hi[:], gu_rest_raw[:]).then_inc(rest_hi_ready, 1)
            for t in range(TB):
                split_h(t)
            act.wait_ge(scales_in, 16 * 5)
            for pair in range(FULL // 2):
                hidden_pair(0, pair, (0, pair + 1) if pair < FULL // 2 - 1 else (1, 0))
                if pair == 0:
                    for t in range(TB, NT):
                        split_h(t)
                else:
                    split_down(pair - 1, P, 2)
            split_down(FULL // 2 - 1, P, 2)
            split_down(FULL // 2, REST, 1)
            gate(0, FULL, 0, bank[6], REST)
            split_act(0, FULL, 0, REST)
            with act.Fori(0, FULL // 2 - 1) as pair:
                hidden_pair(1, pair, (1, pair + 1))
            hidden_pair(1, FULL // 2 - 1, None)
            gate(1, FULL, 0, bank[6], REST)
            split_act(1, FULL, 0, REST)

        @block.vector
        def _(dve):
            def lo(dst, src, hi):
                return nc.vector.tensor_tensor(dst, src, f32(hi), ALU.subtract)

            def tile_squares(tile):
                dve.wait_ge(sq_ready, tile + 1)
                nc.vector.tensor_reduce(sq_sum[:], qk[:], AX_X, ALU.add).then_inc(sq_sum_ready, 1)

            def tile_norm(tile, b, n, from_q, from_kv):
                dve.wait_ge(rstd_ready, tile + 1)
                nc.vector.tensor_tensor(qk[:, 0:GROUP, :], from_q[:].rearrange("p (i d) -> p i d", i=GROUP),
                                        rstd[:, 0:GROUP].unsqueeze(2).broadcast_to([P, GROUP, HD]), ALU.mult)
                dve.wait_ge(v_hi_ready, tile + 1)
                nc.vector.tensor_scalar(qk[:, GROUP, :], from_kv[:, 0:HD], rstd[:, GROUP:GROUP + 1], None,
                                        ALU.mult).then_inc(normed, 1)
                lo(v_lo[:, b, n, :], from_kv[:, HD:KVW], v_hi[:, b, n, :]).then_inc(v_ready, 1)

            def tile_qkT(tile, b, n, from_k):
                dve.wait_ge(qT_hi_ready, tile + 1)
                q = slice(n * P, (n + 1) * P)
                lo(qT_lo[:, b, :, q], tr_bank[1][:].rearrange("p (i q) -> p i q", i=GROUP), qT_hi[:, b, :, q]).then_inc(qT_ready, 1)
                dve.wait_ge(kT_hi_ready, tile + 1)
                nc.vector.scalar_tensor_tensor(kT_lo[:, b, q], from_k[:, KVW:KVW + P], k_scale[:, 0:1], f32(kT_hi[:, b, q]),
                                               ALU.mult, ALU.subtract).then_inc(kT_ready, 1)

            def add_bias(k, n, i):
                wait_apart(dve, scores_done, 4 * k + i + 1)
                nc.vector.tensor_tensor_reduce(out=probs[:, COL[i]:COL[i] + WIDTH[i]], in0=score_bank[i % 2][:, 0:WIDTH[i]],
                                               in1=neg_bias[:, n, SEQ - WIDTH[i]:SEQ], scale=1.0, scalar=HUGE,
                                               op0=ALU.add, op1=ALU.min, accum_out=neg_max[:, i:i + 1]).then_inc(biased, 1)

            def invert(k, half):
                dve.wait_ge(exp_done, 4 * k + 2 * half + 2)
                two = slice(2 * half, 2 * half + 2)
                nc.vector.reciprocal(row_inv[:, two], row_sum[:, two]).then_inc(inv_ready, 1)

            def norm_widest(k):
                dve.wait_ge(inv_ready, 2 * k + 2)
                cols = probs[:, COL[3]:COL[3] + WIDTH[3]]
                nc.vector.tensor_scalar(cols, cols, row_inv[:, 3:4], None, ALU.mult).then_inc(probs3_ready, 1)

            def split_q(g):
                dve.wait_ge(qw_hi_ready, g + 1)
                lo(wq_lo[:].rearrange("p c n -> p (c n)"), stage_q,
                   wq_hi[:].rearrange("p c n -> p (c n)")).then_inc(qw_ready, 1)

            def add_attention(tile, t, from_bank=wo_bank):
                dve.wait_ge(wo_done, tile + 1)
                nc.vector.tensor_tensor(h[:, t, :], from_bank[:], h[:, t, :], ALU.add).then_inc(added, 1)

            def split_pT(k, which):
                dve.wait_ge(pT_hi_ready, 3 * k + which + 1)
                cols = slice(BANK_COL[which], BANK_COL[which] + BANK_WIDTH[which])
                lo(pT_lo[:, cols], tr_bank[which % 2][:, 0:BANK_WIDTH[which]], pT_hi[:, cols]).then_inc(pT_ready, 1)

            def statistics(tile, s, src):
                nc.vector.bn_stats(ln_stats[:, s, :], src).then_inc(stats_ready, 1)
                dve.wait_ge(stats_ready, tile + 1)
                nc.vector.bn_aggr(ln_mean_var[:, s, :], ln_stats[:, s, :]).then_inc(var_ready, 1)

            def normalize(tile, s, dst, src):
                dve.wait_ge(ln_rstd_ready, tile + 1)
                return nc.vector.tensor_scalar(dst, src, ln_mean_var[:, s, 0:1], ln_rstd[:, s, :], ALU.subtract, ALU.mult)

            def scan(step):
                dve.wait_ge(scan_in, 16 * step + 16)
                nc.vector.tensor_reduce(scan_max[:, bass.ds(step, 1)], scan_raw[:], AX_X, ALU.max, apply_absolute_value=True).then_inc(scanned, 1)

            def h_statistics(t):
                dve.wait_ge(added, TILES - NT + t + 1)
                statistics(t, t % 2, h[:, t, :])

            def h_normalize(t):
                normalize(t, t % 2, h[:, t, :], h[:, t, :]).then_inc(ln_done, 1)

            def group(g, first, last):
                for b in range(BATCH):
                    for n in range(GROUP):
                        k = 8 * g + 4 * b + n
                        has_next = has_tile(last, b, n)
                        has_prev = not (first and b == 0)
                        has_scores = not (last and b == 1 and n == GROUP - 1)
                        split_pT(k, 0)
                        split_pT(k, 1)
                        if has_next:
                            tile_squares(k + LEAD)
                        split_pT(k, 2)
                        if has_scores:
                            sn = (n + 1) % GROUP
                            if b == 1 and n == 3:
                                dve.wait_ge(bias_ready, 4 * g + 5)
                            elif b == 0 and n < 3:
                                dve.wait_ge(bias_ready, 4 * g + n + 2)
                            dve.wait_ge(pT_done, 3 * k + 3)
                            add_bias(k + 1, sn, 0)
                            add_bias(k + 1, sn, 1)
                            add_bias(k + 1, sn, 2)
                            invert(k + 1, 0)
                        if has_next:
                            tile_norm(k + LEAD, tile_row(b, n), (n + 1) % TB, q_bank, kv_bank)
                        if has_scores:
                            add_bias(k + 1, sn, 3)
                        dve.wait_ge(oT_hi_ready, k + 1)
                        lo(oT_lo[:, b, n, :], o_bank[:], oT_hi[:, b, n, :]).then_inc(oT_ready, 1)
                        if has_scores:
                            invert(k + 1, 1)
                            norm_widest(k + 1)
                        if has_next:
                            tile_qkT(k + LEAD, tile_row(b, n), (n + 1) % TB, kv_bank)
                        if b == 0 and n == 2 and not last:
                            split_q(g + 1)
                        if has_prev:
                            add_attention(k - 4, TB * (1 - b) + n)
                        scan(k)
                        if last and b == 1:
                            h_statistics(n)
                            if n > 0:
                                h_normalize(n - 1)

            first_q = [q_bank, score_bank[0], score_bank[1], o_bank]
            first_kv = [kv_bank, wo_bank, tr_bank[0], kv_bank]
            raw = h[:].rearrange("p t d -> p (t d)").rearrange("p (c b q) -> p c b q", c=NC, b=BATCH)
            for b in range(BATCH):
                for c in range(NC):
                    dve.wait_ge(xT_hi_ready, NC * b + c + 1)
                    tok = slice(SEQ * b, SEQ * (b + 1))
                    lo(xT_lo[:, c, tok], raw[:, c, b, :], xT_hi[:, c, tok]).then_inc(xT_ready, 1)
                if b == 0:
                    dve.wait_ge(norm_in, 32)
                    nc.vector.scalar_tensor_tensor(k_scale[:], norm_w[:, 0:1], -SCALE, norm_w[:, 1:2],
                                                   ALU.mult, ALU.mult).then_inc(k_scale_ready, 1)
            dve.wait_ge(k_scale_ready, 1)
            for n in range(TB):
                tile_squares(n)
                tile_norm(n, 0, n, first_q[n], first_kv[n])
                tile_qkT(n, 0, n, first_kv[n])
            dve.wait_ge(bias_ready, GROUP)
            add_bias(0, 0, 0)
            add_bias(0, 0, 1)
            tile_squares(TB)
            invert(0, 0)
            add_bias(0, 0, 2)
            add_bias(0, 0, 3)
            tile_norm(TB, 1, 0, q_bank, kv_bank)
            invert(0, 1)
            norm_widest(0)
            tile_qkT(TB, 1, 0, kv_bank)
            dve.wait_ge(x_in, 16)
            group(0, True, False)
            with dve.Fori(1, KV_HEADS - 1) as g:
                group(g, False, False)
            group(KV_HEADS - 1, False, True)

            def split_gu(b, pair, s):
                dve.wait_ge(gu_hi_ready, FULL * b + 2 * pair + s + 1)
                lo(gu_lo[s][:].rearrange("p a c f -> p (a c f)"), gu_raw[s][:].rearrange("p a c f -> p (a c f)"),
                   gu_hi[s][:].rearrange("p a c f -> p (a c f)")).then_inc(gu_ready, 1)

            def split_h(t):
                dve.wait_ge(hT_hi_ready, t + 1)
                tok = slice(t * P, (t + 1) * P)
                lo(hT_lo[:, :, tok], h_bank[t][:].rearrange("p (c q) -> p c q", c=NC), hT_hi[:, :, tok]).then_inc(hT_ready, 1)

            def split_down(pair, rows, chunks):
                dve.wait_ge(down_hi_ready, pair + 1)
                lo(*(a[0:rows, bass.ds(2 * pair, chunks), :].rearrange("p j d -> p (j d)")
                     for a in (down_lo, down_raw, down_hi))).then_inc(down_ready, 1)

            def gate(b, j, s, up_bank, rows):
                dve.wait_ge(silu_ready, NF * b + j + 1)
                dve.wait_ge(up_done, NF * b + j + 1)
                nc.vector.scalar_tensor_tensor(gated[s][0:rows, :], up_bank[0:rows, :], up_scale[0:rows, bass.ds(j, 1)],
                                               silu[s][0:rows, :], ALU.mult, ALU.mult).then_inc(gated_ready, 1)

            def split_act(b, j, s, rows):
                dve.wait_ge(act_hi_ready, NF * b + j + 1)
                part = bass.ds(j, 1)
                lo(act_lo[0:rows, part, :].rearrange("p j q -> p (j q)"), gated[s][0:rows, :],
                   act_hi[0:rows, part, :].rearrange("p j q -> p (j q)")).then_inc(act_ready, 1)

            def hidden_pair(b, pair, next_pair):
                for s in range(2):
                    gate(b, 2 * pair + s, s, bank[2 + s], P)
                    if next_pair is not None:
                        split_gu(*next_pair, s)
                    split_act(b, 2 * pair + s, s, P)

            def output(b):
                if b > 0:
                    dve.wait_ge(y_out, 16 * TB)
                for n in range(TB):
                    tile = TB * b + n
                    dve.wait_ge(y_done, tile + 1)
                    nc.vector.tensor_tensor(y[n], bank[6 + n % 2][:], down_scale[:], ALU.mult).then_inc(y_scaled, 1)
                    dve.wait_ge(y_scaled, tile + 1)
                    nc.vector.tensor_tensor(y[n], y[n], h[:, tile, :], ALU.add).then_inc(y_added, 1)
                    dve.wait_ge(y_added, tile + 1)
                    statistics(NT + tile, n % 2, y[n])
                    normalize(NT + tile, n % 2, y[n], y[n]).then_inc(y_ready, 1)

            h_normalize(TB - 1)
            dve.wait_ge(scanned, STEPS)
            nc.vector.tensor_reduce(row_max[:], scan_max[:], AX_X, ALU.max).then_inc(row_max_ready, 1)
            for s in range(2):
                split_gu(0, 0, s)
            add_attention(TILES - 4, TB, tail_bank[0])
            h_statistics(TB)
            for t in range(TB - 1):
                split_h(t)
            dve.wait_ge(row_max_done, 1)
            nc.vector.tensor_reduce(weight_max[:], score_bank[0][0:1, 0:P], AX_X, ALU.max).then_inc(weight_max_ready, 1)
            dve.wait_ge(weight_max_ready, 1)
            nc.vector.tensor_scalar(narrow[:], weight_max[:], NARROW, None, ALU.is_le).then_inc(narrow_ready, 1)
            add_attention(TILES - 3, TB + 1, tail_bank[1])
            h_statistics(TB + 1)
            h_normalize(TB)
            split_h(TB - 1)
            for n in range(2, GROUP):
                add_attention(TILES - 4 + n, TB + n, tail_bank[n % 2])
                h_statistics(TB + n)
                h_normalize(TB + n - 1)
            dve.wait_ge(rest_hi_ready, 1)
            lo(gu_rest_lo[:].rearrange("p a c f -> p (a c f)"), gu_rest_raw[:].rearrange("p a c f -> p (a c f)"),
               gu_rest_hi[:].rearrange("p a c f -> p (a c f)")).then_inc(rest_ready, 1)
            h_normalize(NT - 1)
            dve.wait_ge(scales_in, 16 * 5)
            hidden_pair(0, 0, (0, 1))
            for t in range(TB, NT):
                split_h(t)
            with dve.Fori(1, FULL // 2 - 1) as pair:
                hidden_pair(0, pair, (0, pair + 1))
                split_down(pair - 1, P, 2)
            hidden_pair(0, FULL // 2 - 1, (1, 0))
            for pair in range(FULL // 2 - 2, FULL // 2):
                split_down(pair, P, 2)
            split_down(FULL // 2, REST, 1)
            gate(0, FULL, 0, bank[7], REST)
            split_act(0, FULL, 0, REST)
            output(0)
            with dve.Fori(0, FULL // 2 - 1) as pair:
                hidden_pair(1, pair, (1, pair + 1))
            hidden_pair(1, FULL // 2 - 1, None)
            gate(1, FULL, 0, bank[7], REST)
            split_act(1, FULL, 0, REST)
            output(1)

        @block.gpsimd
        def _(pool):
            nc.gpsimd.memset(minus_half[:], -0.5).then_inc(consts, 1)
            nc.gpsimd.memset(rms_eps[:], RMS_EPS * HD).then_inc(consts_made, 1)
            nc.gpsimd.memset(ident[:], 1.0).then_inc(consts_made, 1)
            pool.wait_ge(consts_made, 2)
            nc.gpsimd.affine_select(ident[:], ident[:], pattern=[[-1, P]], compare_op=ALU.is_equal, fill=0.0,
                                    base=0, channel_multiplier=1).then_inc(consts, 1)

            def lo(dst, src, hi):
                return nc.gpsimd.tensor_tensor(dst, src, f32(hi), ALU.subtract)

            def split_kv(g):
                pool.wait_ge(kvw_hi_ready, g + 1)
                lo(wkv_lo[:].rearrange("p c n -> p (c n)"), stage_kv,
                   wkv_hi[:].rearrange("p c n -> p (c n)")).then_inc(kvw_ready, 1)

            def split_q(g):
                pool.wait_ge(qw_hi_ready, g + 1)
                lo(wq_lo[:].rearrange("p c n -> p (c n)"), stage_q,
                   wq_hi[:].rearrange("p c n -> p (c n)")).then_inc(qw_ready, 1)

            def split_o(g):
                pool.wait_ge(wow_hi_ready, g + 1)
                lo(wo_lo[:].rearrange("p c n -> p (c n)"), stage_q,
                   wo_hi[:].rearrange("p c n -> p (c n)")).then_inc(wow_ready, 1)

            def tile_rstd(tile):
                pool.wait_ge(sq_sum_ready, tile + 1)
                nc.gpsimd.tensor_tensor(sq_mean[:], sq_sum[:], rms_eps[:], ALU.add).then_inc(mean_ready, 1)
                pool.wait_ge(mean_ready, tile + 1)
                nc.gpsimd.tensor_tensor(rstd[:], sq_mean[:], minus_half[:, 0:GROUP + 1], ALU.pow).then_inc(rstd_ready, 1)

            def norm_probs(k, i):
                wait_apart(pool, inv_ready, 2 * k + 1 + i // 2)
                cols = probs[:, COL[i]:COL[i] + WIDTH[i]]
                nc.gpsimd.tensor_scalar(cols, cols, row_inv[:, i:i + 1], 0.0, ALU.mult, ALU.add).then_inc(probs_ready, 1)

            def layer_rstd(tile, s):
                wait_apart(pool, var_ready, tile + 1)
                nc.gpsimd.tensor_scalar(ln_var_eps[:, s, :], ln_mean_var[:, s, 1:2], 1.0, LN_EPS, ALU.mult, ALU.add).then_inc(var_eps_ready, 1)
                pool.wait_ge(var_eps_ready, tile + 1)
                nc.gpsimd.tensor_tensor(ln_rstd[:, s, :], ln_var_eps[:, s, :], minus_half[:, 0:1], ALU.pow).then_inc(ln_rstd_ready, 1)

            def group(g, last):
                for b in range(BATCH):
                    for n in range(GROUP):
                        k = 8 * g + 4 * b + n
                        has_scores = not (last and b == 1 and n == GROUP - 1)
                        if has_tile(last, b, n):
                            tile_rstd(k + LEAD)
                        if has_scores:
                            norm_probs(k + 1, 0)
                            norm_probs(k + 1, 1)
                            norm_probs(k + 1, 2)
                        if b == 1 and not last:
                            wait_apart(pool, biased, 4 * k + 4)
                            nc.gpsimd.tensor_scalar(neg_bias[:, n, :], neg_bias[:, n, :], 0.5, 0.0, ALU.mult, ALU.add).then_inc(bias_ready, 1)
                        if b == 0 and n == 2 and not last:
                            split_kv(g + 1)
                        if b == 0 and n == 3:
                            split_o(g)
                        if last and b == 1:
                            layer_rstd(n, n % 2)

            split_kv(0)
            split_q(0)
            for i in range(GROUP):
                bias = neg_bias[:, i, :]
                nc.gpsimd.iota(bias, [[-1, SEQ]], base=SEQ - P, channel_multiplier=1,
                               allow_small_or_imprecise_dtypes=True).then_inc(consts_made, 1)
                pool.wait_ge(consts_made, 2 * i + 3)
                nc.gpsimd.tensor_scalar(bias, bias, SLOPES[i], None, ALU.mult).then_inc(consts_made, 1)
                pool.wait_ge(consts_made, 2 * i + 4)
                nc.gpsimd.affine_select(bias, bias, pattern=[[-1, SEQ]], compare_op=ALU.is_ge, fill=MASKED,
                                        base=SEQ - P, channel_multiplier=1).then_inc(bias_ready, 1)
            for n in range(TB + 1):
                tile_rstd(n)
            for i in range(3):
                norm_probs(0, i)
            group(0, False)
            with pool.Fori(1, KV_HEADS - 1) as g:
                group(g, False)

            group(KV_HEADS - 1, True)
            for t in range(TB, NT):
                layer_rstd(t, t % 2)
            with pool.Fori(0, NT // 2) as pair:
                for s in range(2):
                    layer_rstd(NT + 2 * pair + s, s)


def kernel(L0_attn_x, L0_attn_Wq, L0_attn_Wk, L0_attn_Wv, L0_attn_Wo, L0_attn_q_norm_w, L0_attn_k_norm_w,
           L0_ffn_gate_w, L0_ffn_gate_s, L0_ffn_up_w, L0_ffn_up_s, L0_ffn_down_w, L0_ffn_down_s):
    import numpy as np
    import concourse.bacc as bacc
    from concourse.bass_utils import run_bass_kernel_spmd

    def chunked(w, groups):
        w = np.asarray(w).reshape(groups, -1, NC, P)
        return np.ascontiguousarray(w.transpose(0, 3, 2, 1)).reshape(groups, P, -1)

    def hidden_rows(gate, up):
        both = np.stack([gate, up]).reshape(2, -1, min(P, gate.shape[0]), NC, P)
        return np.ascontiguousarray(both.transpose(1, 4, 0, 3, 2)).reshape(both.shape[1], P, -1)

    x = np.asarray(L0_attn_x).reshape(TOK, DM)
    wk = np.asarray(L0_attn_Wk).reshape(KV_HEADS, HD, DM)
    wv = np.asarray(L0_attn_Wv).reshape(KV_HEADS, HD, DM)
    wo = np.asarray(L0_attn_Wo).reshape(DM, KV_HEADS, GROUP, HD)
    gate, up, down = (np.asarray(a) for a in (L0_ffn_gate_w, L0_ffn_up_w, L0_ffn_down_w))
    gate_s, up_s = np.asarray(L0_ffn_gate_s), np.asarray(L0_ffn_up_s)
    arrays = {
        "xT": np.ascontiguousarray(x.reshape(TOK, NC, P).transpose(2, 1, 0)).reshape(P, NC * TOK),
        "x": x,
        "wq": chunked(L0_attn_Wq, KV_HEADS),
        "wkv": chunked(np.concatenate([wk, wv], axis=1), KV_HEADS),
        "wo": np.ascontiguousarray(wo.transpose(1, 3, 2, 0)).reshape(KV_HEADS, HD, GROUP * DM),
        "q_norm": np.asarray(L0_attn_q_norm_w).reshape(HD, 1),
        "k_norm": np.asarray(L0_attn_k_norm_w).reshape(HD, 1),
        "gate_up": hidden_rows(gate[:FULL * P], up[:FULL * P]),
        "gate_up_rest": hidden_rows(gate[FULL * P:], up[FULL * P:])[0],
        "down": np.ascontiguousarray(down[:, :FULL * P].T).reshape(FULL, P, DM),
        "down_rest": np.ascontiguousarray(down[:, FULL * P:].T),
        "gate_s": np.ascontiguousarray(gate_s[:FULL * P].reshape(FULL, P).T),
        "gate_s_rest": gate_s[FULL * P:].reshape(REST, 1),
        "up_s": np.ascontiguousarray(up_s[:FULL * P].reshape(FULL, P).T),
        "up_s_rest": up_s[FULL * P:].reshape(REST, 1),
        "down_s": np.asarray(L0_ffn_down_s),
        "ffn_weights": np.stack([gate, up, down.reshape(gate.shape)]).reshape(STEPS, P, SCAN),
    }
    arrays = {name: np.ascontiguousarray(a) for name, a in arrays.items()}
    nc = bacc.Bacc("TRN2", target_bir_lowering=False, num_devices=1)
    ins = [nc.dram_tensor(name, a.shape, mybir.dt.from_np(a.dtype), kind="ExternalInput").ap() for name, a in arrays.items()]
    out = nc.dram_tensor("out", (NT, P, DM), F32, kind="ExternalOutput").ap()
    block_kernel(nc, *ins, out)
    result = run_bass_kernel_spmd(nc, [arrays], core_ids=[0])
    return result.results[0]["out"].reshape(BATCH, SEQ, DM)
```

```python
import math
from contextlib import ExitStack

import concourse.bass as bass
from concourse import mybir

F32 = mybir.dt.float32
F32R = mybir.dt.float32r
I32 = mybir.dt.int32
ALU = mybir.AluOpType
ACT = mybir.ActivationFunctionType
AX_X = mybir.AxisListType.X

P = 128
BATCH, SEQ, DM = 2, 512, 512
TOK = BATCH * SEQ
HEADS, KV_HEADS, HD = 32, 8, 128
GROUP = HEADS // KV_HEADS
DFF = 1376
NT = TOK // P
TB = SEQ // P
NC = DM // P
QW = GROUP * HD
KVW = 2 * HD
TILES = KV_HEADS * NT
FULL = DFF // P
REST = DFF - FULL * P
NF = FULL + 1
RMS_EPS, LN_EPS = 1e-6, 1e-5
SCALE = HD / math.sqrt(HD)
SLOPE0 = 2 ** (-2 ** (-(math.log2(HEADS) - 3)))
SLOPES = [SLOPE0 * SLOPE0 ** i for i in range(GROUP)]
MASKED = 1e30 * 2 ** KV_HEADS
HUGE = 3.0e38
STEPS = KV_HEADS * BATCH * GROUP
SCAN = 3 * DFF * DM // (P * STEPS)
NARROW = 2.0 ** 12

WIDTH = [P * (i + 1) for i in range(TB)]
COL = [sum(WIDTH[:i]) for i in range(TB)]
SCORES = sum(WIDTH)
BANKS = [[0], [1, 3], [2]]
PT_COL = {0: 0, 1: SEQ, 3: SEQ + 384, 2: 2 * SEQ}
PT_WIDTH = {j: SEQ - P * j for j in range(TB)}
BANK_COL = [0, SEQ, 2 * SEQ]
BANK_WIDTH = [sum(PT_WIDTH[j] for j in bank) for bank in BANKS]


def block_kernel(nc, xT, x, wq, wkv, wo, q_norm, k_norm, gate_up, gate_up_rest, down, down_rest,
                 gate_s, gate_s_rest, up_s, up_s_rest, down_s, ffn_weights, out):
    ctx = ExitStack()
    with ctx:
        def sem(name):
            return ctx.enter_context(nc.semaphore(name))

        def f32(ap):
            return ap.bitcast(F32)

        def tensor(stack, name, shape, dt=F32):
            return stack.enter_context(nc.sbuf_tensor(name, shape, dt))

        h = tensor(ctx, "h", [P, NT, DM])
        ident = tensor(ctx, "ident", [P, P])
        rms_eps = tensor(ctx, "rms_eps", [P, GROUP + 1])
        minus_half = tensor(ctx, "minus_half", [P, GROUP + 1])
        ln_stats = tensor(ctx, "ln_stats", [P, 2, 6])
        ln_small = tensor(ctx, "ln_small", [P, 2, 4])
        ln_mean_var, ln_var_eps, ln_rstd = ln_small[:, :, 0:2], ln_small[:, :, 2:3], ln_small[:, :, 3:4]
        scan_raw = tensor(ctx, "scan_raw", [P, SCAN], I32)
        scan_max = tensor(ctx, "scan_max", [P, STEPS])
        row_max = tensor(ctx, "row_max", [P, 1])
        weight_max = tensor(ctx, "weight_max", [1, 1])
        narrow = tensor(ctx, "narrow", [1, 1], I32)

        attn = ExitStack()
        stage = tensor(attn, "stage", [P, NC * (KVW + QW)])
        stage_kv, stage_q = stage[:, 0:NC * KVW], stage[:, NC * KVW:]
        wkv_hi = tensor(attn, "wkv_hi", [P, NC, KVW], F32R)
        wkv_lo = tensor(attn, "wkv_lo", [P, NC, KVW], F32R)
        wq_hi = tensor(attn, "wq_hi", [P, NC, QW], F32R)
        wq_lo = tensor(attn, "wq_lo", [P, NC, QW], F32R)
        xT_hi = tensor(attn, "xT_hi", [P, NC, TOK], F32R)
        xT_lo = tensor(attn, "xT_lo", [P, NC, TOK], F32R)
        wo_hi = tensor(attn, "wo_hi", [P, GROUP, DM], F32R)
        wo_lo = tensor(attn, "wo_lo", [P, GROUP, DM], F32R)
        qT_hi = tensor(attn, "qT_hi", [P, BATCH, GROUP, SEQ], F32R)
        qT_lo = tensor(attn, "qT_lo", [P, BATCH, GROUP, SEQ], F32R)
        kT_hi = tensor(attn, "kT_hi", [P, BATCH, SEQ], F32R)
        kT_lo = tensor(attn, "kT_lo", [P, BATCH, SEQ], F32R)
        v_hi = tensor(attn, "v_hi", [P, BATCH, TB, HD], F32R)
        v_lo = tensor(attn, "v_lo", [P, BATCH, TB, HD], F32R)
        oT_hi = tensor(attn, "oT_hi", [P, BATCH, GROUP, SEQ], F32R)
        oT_lo = tensor(attn, "oT_lo", [P, BATCH, GROUP, SEQ], F32R)
        probs = tensor(attn, "probs", [P, SCORES])
        pT_hi = tensor(attn, "pT_hi", [P, SCORES], F32R)
        pT_lo = tensor(attn, "pT_lo", [P, SCORES], F32R)
        neg_bias = tensor(attn, "neg_bias", [P, GROUP, SEQ])
        qk = tensor(attn, "qk", [P, GROUP + 1, HD])
        neg_max = tensor(attn, "neg_max", [P, TB])
        row_sum = tensor(attn, "row_sum", [P, TB])
        sq_sum = tensor(attn, "sq_sum", [P, TB, GROUP + 1])
        rstd = tensor(attn, "rstd", [P, TB, GROUP + 1])
        norm_w = tensor(attn, "norm_w", [P, 3])
        k_scale = norm_w[:, 2:3]
        first_qk = [a.rearrange("p (i d) -> p i d", i=GROUP + 1) for a in (
            qk[:].rearrange("p i d -> p (i d)"), probs[:, 0:SCORES // 2], probs[:, SCORES // 2:], h[:].rearrange("p t d -> p (t d)")[:, 0:SCORES // 2])]
        attn.close()

        ffn = ExitStack()
        gu_raw = [tensor(ffn, f"gu_raw{s}", [P, 2, NC, P], I32) for s in range(2)]
        gu_rest_raw = tensor(ffn, "gu_rest_raw", [P, 2, NC, REST], I32)
        gate_scale = tensor(ffn, "gate_scale", [P, NF])
        up_scale = tensor(ffn, "up_scale", [P, NF])
        down_scale = tensor(ffn, "down_scale", [P, DM])
        gu_hi = [tensor(ffn, f"gu_hi{s}", [P, 2, NC, P], F32R) for s in range(2)]
        gu_lo = [tensor(ffn, f"gu_lo{s}", [P, 2, NC, P], F32R) for s in range(2)]
        gu_rest_hi = tensor(ffn, "gu_rest_hi", [P, 2, NC, REST], F32R)
        gu_rest_lo = tensor(ffn, "gu_rest_lo", [P, 2, NC, REST], F32R)
        hT_hi = tensor(ffn, "hT_hi", [P, NC, TOK], F32R)
        hT_lo = tensor(ffn, "hT_lo", [P, NC, TOK], F32R)
        act_hi = tensor(ffn, "act_hi", [P, NF, SEQ], F32R)
        act_lo = tensor(ffn, "act_lo", [P, NF, SEQ], F32R)
        down_raw = tensor(ffn, "down_raw", [P, NF, DM], I32)
        down_hi = tensor(ffn, "down_hi", [P, NF, DM], F32R)
        down_lo = tensor(ffn, "down_lo", [P, NF, DM], F32R)
        silu = [tensor(ffn, f"silu{s}", [P, SEQ]) for s in range(2)]
        gated = [tensor(ffn, f"gated{s}", [P, SEQ]) for s in range(2)]
        y = [down_raw[:, n, :].bitcast(F32) for n in range(TB)]
        ffn.close()

        bank = [ctx.enter_context(nc.psum_tensor(f"bank{i}", [P, 512], F32)) for i in range(8)]
        score_bank = bank[0:2]
        q_bank, kv_bank, o_bank, wo_bank = bank[2], bank[3], bank[6], bank[7]
        tr_bank = bank[4:6]
        first_q = [score_bank[0], score_bank[1], tr_bank[1], o_bank]
        first_kv = [kv[:, c:c + KVW] for kv in (wo_bank, tr_bank[0]) for c in (0, KVW)]
        first_k, first_v = [kv[:, 0:HD] for kv in first_kv], [kv[:, HD:KVW] for kv in first_kv]
        first_kT = [kv[:].rearrange("p (n c) -> p n c", n=2)[:, :, 0:P] for kv in (wo_bank, tr_bank[0])]
        tail_bank = [wo_bank, o_bank]
        y_bank = bank[4:6]
        h_bank = [bank[i] for i in (4, 5, 1, 3, 4, 5, 6, 7)]

        x_in, kv_in, q_in, wo_in, norm_in = (sem(f"{n}_in") for n in ("x", "kv", "q", "wo", "norm"))
        kv0_in, q0_in = ([sem(f"{n}0_in{half}") for half in range(2)] for n in ("kv", "q"))
        xT0_in, xT1_in = [sem(f"xT0_in{c}") for c in range(NC)], sem("xT1_in")
        rest_in, scales_in, y_out = (sem(n) for n in ("rest_in", "scales_in", "y_out"))
        gu_in = [sem(f"gu_in{s}") for s in range(2)]
        down_in = [sem(f"down_in{pair}") for pair in range(FULL // 2 + 1)]
        consts_made = sem("consts_made")
        apart = sem("apart")
        consts, bias_ready, k_scale_ready = sem("consts"), sem("bias_ready"), sem("k_scale_ready")
        xT_hi_ready, xT_ready = sem("xT_hi_ready"), sem("xT_ready")
        kvw_hi_ready, kvw_ready = sem("kvw_hi_ready"), sem("kvw_ready")
        qw_hi_ready, qw_ready = sem("qw_hi_ready"), sem("qw_ready")
        wow_hi_ready, wow_ready = sem("wow_hi_ready"), sem("wow_ready")
        kv_done, q_done, v_hi_ready, v_ready = sem("kv_done"), sem("q_done"), sem("v_hi_ready"), sem("v_ready")
        sq_ready, sq_sum_ready, mean_ready, rstd_ready = sem("sq_ready"), sem("sq_sum_ready"), sem("mean_ready"), sem("rstd_ready")
        normed, qT_done, kT_done = sem("normed"), sem("qT_done"), sem("kT_done")
        qT_hi_ready, kT_hi_ready, qT_ready, kT_ready = sem("qT_hi_ready"), sem("kT_hi_ready"), sem("qT_ready"), sem("kT_ready")
        scores_done, biased, exp_done, inv_ready, probs_ready, probs3_ready = (
            sem(n) for n in ("scores_done", "biased", "exp_done", "inv_ready", "probs_ready", "probs3_ready"))
        pT_done, pT_hi_ready, pT_ready = sem("pT_done"), sem("pT_hi_ready"), sem("pT_ready")
        o_done, oT_hi_ready, oT_ready = sem("o_done"), sem("oT_hi_ready"), sem("oT_ready")
        wo_done, added = sem("wo_done"), sem("added")
        stats_ready, var_ready, var_eps_ready, ln_rstd_ready, ln_done = (
            sem(n) for n in ("stats_ready", "var_ready", "var_eps_ready", "ln_rstd_ready", "ln_done"))
        hT_done, hT_hi_ready, hT_ready = sem("hT_done"), sem("hT_hi_ready"), sem("hT_ready")
        scan_in, scanned, row_max_ready, row_max_done, weight_max_ready, narrow_ready = (
            sem(n) for n in ("scan_in", "scanned", "row_max_ready", "row_max_done", "weight_max_ready", "narrow_ready"))
        gu_hi_ready, gu_ready, rest_hi_ready, rest_ready = (
            sem(n) for n in ("gu_hi_ready", "gu_ready", "rest_hi_ready", "rest_ready"))
        down_hi_ready, down_ready = sem("down_hi_ready"), sem("down_ready")
        gate_done, up_done, silu_ready, gated_ready = sem("gate_done"), sem("up_done"), sem("silu_ready"), sem("gated_ready")
        act_hi_ready, act_ready = sem("act_hi_ready"), sem("act_ready")
        y_done, y_scaled, y_added, y_ready = sem("y_done"), sem("y_scaled"), sem("y_added"), sem("y_ready")

        def wait(engine, semaphore, value):
            if not isinstance(value, int) or value > 0:
                engine.wait_ge(semaphore, value)

        def wait_apart(engine, semaphore, value):
            engine.wait_ge(semaphore, value)
            engine.sem_inc(apart, 1)

        block = ctx.enter_context(nc.Block())

        @block.sync
        def _(sp):
            raw, src = (a.rearrange("p (c b q) -> p c b q", c=NC, b=BATCH) for a in (h[:].rearrange("p t d -> p (t d)"), xT))
            for half in range(2):
                cols = slice(half * NC * KVW // 2, (half + 1) * NC * KVW // 2)
                for c in (2 * half, 2 * half + 1):
                    sp.dma_start(raw[:, c, 0, :], src[:, c, 0, :]).then_inc(xT0_in[c], 16)
                    if c % 2 == 0:
                        sp.dma_start(stage_kv[:, cols], wkv[0, :, cols]).then_inc(kv0_in[half], 16)
            for half in range(2):
                cols = slice(half * NC * QW // 2, (half + 1) * NC * QW // 2)
                sp.dma_start(stage_q[:, cols], wq[0, :, cols]).then_inc(q0_in[half], 16)
            sp.dma_start(norm_w[:, 0:1], q_norm).then_inc(norm_in, 16)
            sp.dma_start(norm_w[:, 1:2], k_norm).then_inc(norm_in, 16)
            sp.dma_start(raw[:, :, 1, :], src[:, :, 1, :]).then_inc(xT1_in, 16)
            sp.wait_ge(kT_done, TB)
            sp.dma_start(h[:], x.rearrange("(t p) d -> p t d", p=P)).then_inc(x_in, 16)
            sp.wait_ge(kvw_ready, NC)
            sp.dma_start(stage_kv, wkv[1, :, :]).then_inc(kv_in, 16)
            sp.wait_ge(qw_ready, NC)
            sp.dma_start(stage_q, wq[1, :, :]).then_inc(q_in, 16)
            sp.dma_start(scan_raw[:], ffn_weights[0, :, :]).then_inc(scan_in, 16)

            def load_scan(step):
                sp.wait_ge(scanned, step + 1)
                sp.dma_start(scan_raw[:], ffn_weights[bass.ds(step + 1, 1), :, :].rearrange("s p n -> (s p) n")).then_inc(scan_in, 16)

            def load_group(g, kv, q):
                for n in range(2):
                    load_scan(8 * g + n)
                sp.wait_ge(qw_ready, NC * (g + 2))
                sp.dma_start(stage_q, wo[bass.ds(g, 1), :, :].rearrange("g p n -> (g p) n")).then_inc(wo_in, 16)
                if kv:
                    sp.wait_ge(kvw_ready, NC * (g + 2))
                    sp.dma_start(stage_kv, wkv[bass.ds(g + 2, 1), :, :].rearrange("g p n -> (g p) n")).then_inc(kv_in, 16)
                for n in range(2, 4):
                    load_scan(8 * g + n)
                sp.wait_ge(wow_ready, g + 1)
                sp.dma_start(stage_q, q[bass.ds(g + 2 if kv else g + 1, 1), :, :].rearrange("g p n -> (g p) n")).then_inc(q_in if kv else wo_in, 16)
                for n in range(4, 8):
                    load_scan(8 * g + n)

            with sp.Fori(0, KV_HEADS - 2) as g:
                load_group(g, True, wq)
            load_group(KV_HEADS - 2, False, wo)
            for n in range(4):
                load_scan(STEPS - 8 + n)
            sp.wait_ge(wow_ready, KV_HEADS)
            sp.wait_ge(q_done, TILES)
            sp.dma_start(gu_rest_raw[:].rearrange("p a c f -> p (a c f)"), gate_up_rest).then_inc(rest_in, 16)

            def load_pair(b, pair):
                for s in range(2):
                    wait(sp, gu_ready, FULL * b + 2 * pair + s - 1)
                    sp.dma_start(gu_raw[s][:].rearrange("p a c f -> p (a c f)"),
                                 gate_up[bass.ds(2 * pair + s, 1), :, :].rearrange("j p n -> (j p) n")).then_inc(gu_in[s], 16)

            load_pair(0, 0)
            sp.dma_start(gate_scale[:, 0:FULL], gate_s).then_inc(scales_in, 16)
            sp.dma_start(gate_scale[0:REST, FULL:NF], gate_s_rest).then_inc(scales_in, 16)
            sp.dma_start(up_scale[:, 0:FULL], up_s).then_inc(scales_in, 16)
            sp.dma_start(up_scale[0:REST, FULL:NF], up_s_rest).then_inc(scales_in, 16)
            sp.dma_start(down_scale[:], down_s.partition_broadcast(P)).then_inc(scales_in, 16)
            for n in range(4, 7):
                load_scan(STEPS - 8 + n)
            sp.wait_ge(added, TILES)
            for pair in range(1, FULL // 2 + 1):
                if pair < FULL // 2:
                    load_pair(0, pair)
                sp.dma_start(down_raw[:, 2 * pair - 2:2 * pair, :],
                             down[2 * pair - 2:2 * pair, :, :].rearrange("j p d -> p j d")).then_inc(down_in[pair - 1], 16)
            sp.dma_start(down_raw[0:REST, FULL, :], down_rest).then_inc(down_in[FULL // 2], 16)
            load_pair(1, 0)
            with sp.Fori(1, FULL // 2) as pair:
                load_pair(1, pair)
            for t in range(NT):
                sp.wait_ge(y_ready, t + 1)
                sp.dma_start(out[t, :, :], y[t % TB]).then_inc(y_out, 16)
            sp.wait_ge(y_out, 16 * NT)

        LEAD = 5

        def has_tile(last, b, n):
            return not last or 4 * b + n + LEAD < NT

        def is_short(first, last, b, n):
            return first and b == 0 or not has_tile(last, b, n)

        def pT_bank(which, first, last, b, n):
            if which == 2 and is_short(first, last, b, n):
                return wo_bank if first else q_bank
            return tr_bank[which % 2]

        def pT_order(first, last, b, n):
            return (0, 2, 1) if is_short(first, last, b, n) else (0, 1, 2)

        def tile_row(b, n):
            return 1 - b if n < 3 else b

        @block.tensor
        def _(pe):
            def product(dst, a_hi, a_lo, b_hi, b_lo, first, last):
                nc.tensor.matmul(dst, a_hi, b_lo, start=first, stop=False)
                nc.tensor.matmul(dst, a_lo, b_hi, start=False, stop=False)
                return nc.tensor.matmul(dst, a_hi, b_hi, start=False, stop=last)

            def project_kv_chunk(dst, b, n, c):
                t = slice((TB * b + n) * P, (TB * b + n + 1) * P)
                return product(dst, xT_hi[:, c, t], xT_lo[:, c, t],
                               wkv_hi[:, c, :], wkv_lo[:, c, :], c == 0, c == NC - 1)

            def project_kv(dst, b, n):
                for c in range(NC):
                    last = project_kv_chunk(dst, b, n, c)
                last.then_inc(kv_done, 1)

            def project_q(dst, b, n):
                t = slice((TB * b + n) * P, (TB * b + n + 1) * P)
                for c in range(NC):
                    last = product(dst[:], xT_hi[:, c, t], xT_lo[:, c, t],
                                   wq_hi[:, c, :], wq_lo[:, c, :], c == 0, c == NC - 1)
                last.then_inc(q_done, 1)

            def transpose_q(tile, dst, qk):
                pe.wait_ge(normed, tile + 1)
                for i in range(GROUP):
                    last = nc.tensor.transpose(dst[:, i * P:(i + 1) * P], qk[:, i, :], ident[:])
                last.then_inc(qT_done, 1)

            def transpose_k(tile, dst, qk):
                pe.wait_ge(v_ready, tile + 1)
                nc.tensor.transpose(dst, qk[:, GROUP, :], ident[:]).then_inc(kT_done, 1)

            def transpose_qk(tile):
                transpose_q(tile, tr_bank[1], qk)
                transpose_k(tile, kv_bank[:, KVW:KVW + P], qk)

            def scores(k, b, n, i):
                wait(pe, biased, 4 * k + i - 1)
                q = slice(i * P, (i + 1) * P)
                product(score_bank[i % 2][:, 0:WIDTH[i]], qT_hi[:, b, n, q], qT_lo[:, b, n, q],
                        kT_hi[:, b, 0:WIDTH[i]], kT_lo[:, b, 0:WIDTH[i]], True, True).then_inc(scores_done, 1)

            def transpose_probs(k, which, dst):
                for j in BANKS[which]:
                    for i in range(j, TB):
                        if which == 0 and i == TB - 1:
                            pe.wait_ge(probs3_ready, k + 1)
                        col = PT_COL[j] - BANK_COL[which] + (i - j) * P
                        last = nc.tensor.transpose(dst[:, col:col + P],
                                                   probs[:, COL[i] + j * P:COL[i] + (j + 1) * P], ident[:])
                last.then_inc(pT_done, 1)

            def attend(b, j):
                cols = slice(PT_COL[j], PT_COL[j] + PT_WIDTH[j])
                return product(o_bank[:, j * P:SEQ], v_hi[:, b, j, :], v_lo[:, b, j, :],
                               pT_hi[:, cols], pT_lo[:, cols], j == 0, j == 2)

            def project_out(b, n, half, dst):
                q = slice(n * P, (n + 1) * P)
                for i in (2 * half, 2 * half + 1):
                    last = product(dst[:], oT_hi[:, b, i, q], oT_lo[:, b, i, q],
                                   wo_hi[:, i, :], wo_lo[:, i, :], i == 0, i == GROUP - 1)
                if half == 1:
                    last.then_inc(wo_done, 1)

            def group(g, first, last):
                for b in range(BATCH):
                    for n in range(GROUP):
                        k = 8 * g + 4 * b + n
                        has_next = has_tile(last, b, n)
                        has_prev = not (first and b == 0)
                        has_scores = not (last and b == 1 and n == GROUP - 1)
                        new_weights = b == 0 and n == 3
                        short = is_short(first, last, b, n)

                        def next_scores(i):
                            if has_scores:
                                sb, sn = (b, n + 1) if n < 3 else (1 - b, 0)
                                if n == 3 and i == 0:
                                    pe.wait_ge(qT_ready, 8 * g + 4 * b + 8)
                                    pe.wait_ge(kT_ready, 8 * g + 4 * b + 8)
                                scores(k + 1, sb, sn, i)

                        def next_q():
                            if has_next:
                                if new_weights:
                                    pe.wait_ge(qw_ready, NC * (g + 2))
                                pe.wait_ge(normed, k + LEAD)
                                project_q(q_bank, tile_row(b, n), (n + 1) % TB)

                        def next_kv():
                            if has_next:
                                if new_weights:
                                    pe.wait_ge(kvw_ready, NC * (g + 2))
                                pe.wait_ge(kT_ready, k + LEAD)
                                project_kv(kv_bank[:, 0:KVW], tile_row(b, n), (n + 1) % TB)

                        def prev_out(half):
                            if has_prev:
                                if n == 0 and half == 0:
                                    pe.wait_ge(oT_ready, 8 * g + 4 * b)
                                    if b == 1:
                                        pe.wait_ge(wow_ready, g + 1)
                                if half == 0:
                                    wait(pe, added, k - 4)
                                project_out(1 - b, n, half, wo_bank)

                        def probs_to_bank(which):
                            transpose_probs(k, which, pT_bank(which, first, last, b, n))

                        pe.wait_ge(probs_ready, 3 * k + 3)
                        wait(pe, pT_ready, 3 * k)
                        probs_to_bank(0)
                        if short:
                            probs_to_bank(2)
                            next_scores(0)
                            next_scores(1)
                        elif not new_weights:
                            next_q()
                        pe.wait_ge(qT_ready, k + LEAD if has_tile(last, b, n - 1) or n == 0 and b == 0 else TILES)
                        probs_to_bank(1)
                        if short:
                            if new_weights:
                                next_kv()
                                next_q()
                            else:
                                next_q()
                                next_kv()
                            prev_out(0)
                            next_scores(2)
                            next_scores(3)
                            prev_out(1)
                        else:
                            next_kv()
                            if new_weights:
                                next_q()
                            pe.wait_ge(pT_ready, 3 * k + 1)
                            probs_to_bank(2)
                            next_scores(0)
                            next_scores(1)
                        pe.wait_ge(pT_ready, 3 * k + 1)
                        wait(pe, oT_ready, k)
                        attend(b, 0)
                        pe.wait_ge(pT_ready, 3 * k + (3 if short else 2))
                        attend(b, 1)
                        attend(b, 3)
                        if not short:
                            next_scores(2)
                            next_scores(3)
                        pe.wait_ge(pT_ready, 3 * k + 3)
                        attend(b, 2).then_inc(o_done, 1)
                        if not short:
                            prev_out(0)
                        if has_next:
                            transpose_qk(k + LEAD)
                        if not short:
                            prev_out(1)

            pe.wait_ge(consts, 2)
            for c in range(NC):
                pe.wait_ge(xT_ready, c + 1)
                pe.wait_ge(kvw_ready, 2 * (c // 2) + 2)
                for n in (0, 2):
                    last = project_kv_chunk(first_kv[n], 0, n, c)
                    if c == NC - 1:
                        last.then_inc(kv_done, 1)
            for n in (1, 3):
                project_kv(first_kv[n], 0, n)
            for n in range(TB):
                if n == 0:
                    pe.wait_ge(qw_ready, NC)
                project_q(first_q[n], 0, n)
                if n == 2:
                    transpose_q(0, first_q[0], first_qk[0])
            transpose_q(1, first_q[1], first_qk[1])
            for n in range(2):
                transpose_k(1, first_k[n], first_qk[n])
            pe.wait_ge(xT_ready, BATCH * NC)
            project_kv(kv_bank[:, 0:KVW], 1, 0)
            transpose_q(2, first_q[2], first_qk[2])
            project_q(q_bank, 1, 0)
            transpose_q(3, first_q[3], first_qk[3])
            for n in range(2, TB):
                transpose_k(TB - 1, first_k[n], first_qk[n])
            pe.wait_ge(qT_ready, 2)
            pe.wait_ge(kT_ready, 2)
            scores(0, 0, 0, 0)
            scores(0, 0, 0, 1)
            pe.wait_ge(qT_ready, TB)
            pe.wait_ge(kT_ready, TB)
            scores(0, 0, 0, 2)
            scores(0, 0, 0, 3)
            transpose_qk(TB)
            group(0, True, False)
            with pe.Fori(1, KV_HEADS - 1) as g:
                group(g, False, False)
            group(KV_HEADS - 1, False, True)

            def transpose_h(t):
                pe.wait_ge(ln_done, t + 1)
                for c in range(NC):
                    last = nc.tensor.transpose(h_bank[t][:, c * P:(c + 1) * P], h[:, t, c * P:(c + 1) * P], ident[:])
                last.then_inc(hT_done, 1)

            for t in range(2):
                transpose_h(t)
            pe.wait_ge(oT_ready, STEPS)
            for n in range(GROUP):
                pe.wait_ge(added, TILES - 4 if n == 0 else TILES - 4 + n - 1)
                project_out(1, n, 0, tail_bank[n % 2])
                project_out(1, n, 1, tail_bank[n % 2])
                if n == 0:
                    transpose_h(2)
                    pe.wait_ge(row_max_ready, 1)
                    nc.tensor.transpose(score_bank[0][0:1, 0:P], row_max[:], ident[:]).then_inc(row_max_done, 1)
                if n == 1:
                    transpose_h(TB - 1)

            def feed_forward(has_lo):
                def hidden(b, banks, weights_hi, weights_lo, rows):
                    tok = slice(SEQ * b, SEQ * (b + 1))
                    for a, done in ((0, gate_done), (1, up_done)):
                        dst = banks[a][0:rows, :]
                        for c in range(NC):
                            nc.tensor.matmul(dst, weights_hi[:, a, c, :], hT_lo[:, c, tok], start=c == 0, stop=False)
                            if has_lo:
                                nc.tensor.matmul(dst, weights_lo[:, a, c, :], hT_hi[:, c, tok], start=False, stop=False)
                            last = nc.tensor.matmul(dst, weights_hi[:, a, c, :], hT_hi[:, c, tok], start=False, stop=c == NC - 1)
                        last.then_inc(done, 1)

                def hidden_pair(b, pair):
                    for s in range(2):
                        pe.wait_ge(gu_ready, FULL * b + 2 * pair + s + 1)
                        wait(pe, gated_ready, NF * b + 2 * pair + s - 1)
                        hidden(b, (bank[s], bank[2 + s]), gu_hi[s], gu_lo[s], P)

                def down_tile(b, n):
                    dst = y_bank[n % 2][:]
                    for j in range(NF):
                        if n == 0:
                            if b == 0 and j % 2 == 0:
                                pe.wait_ge(down_ready, j // 2 + 1)
                            pe.wait_ge(act_ready, NF * b + j + 1)
                        rows = P if j < FULL else REST
                        q = slice(n * P, (n + 1) * P)
                        nc.tensor.matmul(dst, act_lo[0:rows, j, q], down_hi[0:rows, j, :], start=j == 0, stop=False)
                        if has_lo:
                            nc.tensor.matmul(dst, act_hi[0:rows, j, q], down_lo[0:rows, j, :], start=False, stop=False)
                        last = nc.tensor.matmul(dst, act_hi[0:rows, j, q], down_hi[0:rows, j, :], start=False, stop=j == NF - 1)
                    last.then_inc(y_done, 1)

                for b in range(BATCH):
                    pe.wait_ge(hT_ready, TB * b + TB)
                    hidden_pair(b, 0)
                    if b == 0:
                        pe.wait_ge(added, TILES)
                        for t in range(TB, NT):
                            transpose_h(t)
                    with pe.Fori(1, FULL // 2) as pair:
                        hidden_pair(b, pair)
                    pe.wait_ge(rest_ready, 1)
                    if b == 0:
                        pe.wait_ge(hT_ready, NT)
                    hidden(b, bank[6:8], gu_rest_hi, gu_rest_lo, REST)
                    for n in range(TB):
                        wait(pe, y_scaled, TB * b + n - 1)
                        down_tile(b, n)

            pe.wait_ge(narrow_ready, 1)
            is_narrow = pe.value_load(narrow[0:1, 0:1], min_val=0, max_val=1)
            with pe.If(is_narrow == 0):
                feed_forward(True)
            with pe.If(is_narrow == 1):
                feed_forward(False)

        @block.scalar
        def _(act):
            def hi(dst, src):
                return nc.scalar.activation(dst, src, ACT.Copy)

            def split_kv(g, c, chunks):
                wait(act, kv_done, 8 * g)
                if isinstance(g, int) and g == 0:
                    act.wait_ge(kv0_in[c // 2], 16)
                else:
                    act.wait_ge(kv_in, 16 * g)
                hi(wkv_hi[:, c:c + chunks, :].rearrange("p c n -> p (c n)"), stage_kv[:, c * KVW:(c + chunks) * KVW]).then_inc(kvw_hi_ready, chunks)

            def split_q(g, c, chunks):
                wait(act, q_done, 8 * g)
                if isinstance(g, int) and g == 0:
                    act.wait_ge(q0_in[c // 2], 16)
                else:
                    act.wait_ge(q_in, 16 * g)
                hi(wq_hi[:, c:c + chunks, :].rearrange("p c n -> p (c n)"), stage_q[:, c * QW:(c + chunks) * QW]).then_inc(qw_hi_ready, chunks)

            def split_o(g):
                wait(act, wo_done, 8 * g)
                act.wait_ge(wo_in, 16 * g + 16)
                hi(wo_hi[:].rearrange("p c n -> p (c n)"), stage_q).then_inc(wow_hi_ready, 1)

            def k_squares(tile, dst, from_k):
                act.wait_ge(kv_done, tile + 1)
                return nc.scalar.activation(dst[:, GROUP, :], from_k, ACT.Square)

            def q_squares(tile, dst, from_q):
                act.wait_ge(q_done, tile + 1)
                return nc.scalar.activation(dst[:, 0:GROUP, :].rearrange("p i d -> p (i d)"), from_q[:], ACT.Square)

            def tile_squares(tile, transposed, q_last):
                act.wait_ge(kT_done, transposed)
                if q_last:
                    k_squares(tile, qk, kv_bank[:, 0:HD])
                    q_squares(tile, qk, q_bank).then_inc(sq_ready, 1)
                else:
                    q_squares(tile, qk, q_bank)
                    k_squares(tile, qk, kv_bank[:, 0:HD]).then_inc(sq_ready, 1)

            def tile_v(b, n, from_v):
                hi(v_hi[:, b, n, :], from_v).then_inc(v_hi_ready, 1)

            def tile_qT(tile, b, n, from_q):
                act.wait_ge(qT_done, tile + 1)
                hi(qT_hi[:, b, :, n * P:(n + 1) * P], from_q[:].rearrange("p (i q) -> p i q", i=GROUP)).then_inc(qT_hi_ready, 1)

            def tile_kT(tile, b, n, from_k, tiles=1):
                act.wait_ge(kT_done, tile + tiles)
                dst = kT_hi[:, b, n * P:(n + tiles) * P].rearrange("p (t q) -> p t q", t=tiles)
                nc.scalar.activation(dst, from_k, ACT.Copy, scale=k_scale).then_inc(kT_hi_ready, tiles)

            def tile_qkT(tile, b, n):
                tile_qT(tile, b, n, tr_bank[1])
                tile_kT(tile, b, n, kv_bank[:, KVW:KVW + P].unsqueeze(1))

            def exponentials(k, i):
                act.wait_ge(biased, 4 * k + i + 1)
                cols = probs[:, COL[i]:COL[i] + WIDTH[i]]
                nc.scalar.activation(cols, cols, ACT.Exp, bias=neg_max[:, i:i + 1], scale=-1.0,
                                     accum_out=row_sum[:, i:i + 1]).then_inc(exp_done, 1)

            def split_pT(k, nth, which, src):
                act.wait_ge(pT_done, 3 * k + nth + 1)
                hi(pT_hi[:, BANK_COL[which]:BANK_COL[which] + BANK_WIDTH[which]],
                   src[:, 0:BANK_WIDTH[which]]).then_inc(pT_hi_ready, 1)

            def group(g, first, last):
                for b in range(BATCH):
                    for n in range(GROUP):
                        k = 8 * g + 4 * b + n
                        has_next = has_tile(last, b, n)
                        has_scores = not (last and b == 1 and n == GROUP - 1)
                        new_weights = b == 0 and n == 2 and not last
                        short = is_short(first, last, b, n)

                        def next_exponentials(*blocks):
                            for i in blocks if has_scores else ():
                                exponentials(k + 1, i)

                        def next_tile():
                            if has_next:
                                tile_squares(k + LEAD, k + LEAD, b == 0 and n == 3)

                        def next_v():
                            if has_next:
                                tile_v(tile_row(b, n), (n + 1) % TB, kv_bank[:, HD:KVW])

                        wait(act, o_done, k)
                        for nth, which in enumerate(pT_order(first, last, b, n)):
                            if nth == 2 and not short:
                                next_tile()
                            split_pT(k, nth, which, pT_bank(which, first, last, b, n))
                        if short:
                            next_exponentials(0, 1)
                            next_tile()
                        if n < 3:
                            next_v()
                        if short:
                            next_exponentials(2, 3)
                            if b == 0 and n == 3 and last:
                                split_o(g)
                        else:
                            if new_weights:
                                split_kv(g + 1, 0, NC)
                            next_exponentials(0, 1)
                            if new_weights:
                                split_q(g + 1, 0, 1)
                            next_exponentials(2)
                        act.wait_ge(o_done, k + 1)
                        if n == 3:
                            next_v()
                        hi(oT_hi[:, b, n, :], o_bank[:]).then_inc(oT_hi_ready, 1)
                        if not short:
                            if new_weights:
                                split_q(g + 1, 1, 1)
                            next_exponentials(3)
                        if has_next:
                            tile_qkT(k + LEAD, tile_row(b, n), (n + 1) % TB)
                        if new_weights and short:
                            split_kv(g + 1, 0, NC)
                            split_q(g + 1, 0, 2)
                        if new_weights:
                            split_q(g + 1, 2, 2)
                        if b == 0 and n == 3 and not last:
                            split_o(g)

            raw = h[:].rearrange("p t d -> p (t d)").rearrange("p (c b q) -> p c b q", c=NC, b=BATCH)
            for c in range(NC):
                act.wait_ge(xT0_in[c], 16)
                hi(xT_hi[:, c, 0:SEQ], raw[:, c, 0, :]).then_inc(xT_hi_ready, 1)
                if c % 2 == 0:
                    split_kv(0, c, 2)
            split_q(0, 0, 2)
            split_q(0, 2, 2)
            act.wait_ge(xT1_in, 16)
            for c in range(NC):
                hi(xT_hi[:, c, SEQ:TOK], raw[:, c, 1, :]).then_inc(xT_hi_ready, 1)
            for n in range(TB):
                if n == TB - 1:
                    q_squares(0, first_qk[0], first_q[0]).then_inc(sq_ready, 1)
                    act.wait_ge(xT_ready, BATCH * NC)
                k_squares(2 + n // 2, first_qk[n], first_k[n])
                tile_v(0, n, first_v[n])
            for n in range(1, TB):
                q_squares(n, first_qk[n], first_q[n]).then_inc(sq_ready, 1)
                if n == 2:
                    tile_qT(0, 0, 0, first_q[0])
            tile_qT(1, 0, 1, first_q[1])
            act.wait_ge(k_scale_ready, 1)
            tile_kT(0, 0, 0, first_kT[0], 2)
            tile_qT(2, 0, 2, first_q[2])
            tile_squares(TB, 2, True)
            tile_qT(3, 0, 3, first_q[3])
            tile_kT(2, 0, 2, first_kT[1], 2)
            tile_v(1, 0, kv_bank[:, HD:KVW])
            exponentials(0, 0)
            exponentials(0, 1)
            exponentials(0, 2)
            exponentials(0, 3)
            tile_qkT(TB, 1, 0)
            group(0, True, False)
            with act.Fori(1, KV_HEADS - 1) as g:
                group(g, False, False)
            group(KV_HEADS - 1, False, True)

            def split_gu(b, pair, s, multiplied):
                act.wait_ge(gu_in[s], 16 * (FULL // 2 * b + pair + 1))
                wait(act, up_done, multiplied)
                hi(gu_hi[s][:], gu_raw[s][:]).then_inc(gu_hi_ready, 1)

            def split_down(pair, rows, chunks):
                act.wait_ge(down_in[pair], 16)
                part = slice(2 * pair, 2 * pair + chunks)
                hi(down_hi[0:rows, part, :], down_raw[0:rows, part, :]).then_inc(down_hi_ready, 1)

            def split_h(t):
                act.wait_ge(hT_done, t + 1)
                hi(hT_hi[:, :, t * P:(t + 1) * P], h_bank[t][:].rearrange("p (c q) -> p c q", c=NC)).then_inc(hT_hi_ready, 1)

            def gate(b, j, s, gate_bank, rows):
                act.wait_ge(gate_done, NF * b + j + 1)
                nc.scalar.activation(silu[s][0:rows, :], gate_bank[0:rows, :], ACT.Silu,
                                     scale=gate_scale[0:rows, bass.ds(j, 1)]).then_inc(silu_ready, 1)

            def split_act(b, j, s, rows):
                act.wait_ge(gated_ready, NF * b + j + 1)
                hi(act_hi[0:rows, bass.ds(j, 1), :].rearrange("p j q -> p (j q)"), gated[s][0:rows, :]).then_inc(act_hi_ready, 1)

            def hidden_pair(b, pair, next_pair):
                for s in range(2):
                    gate(b, 2 * pair + s, s, bank[s], P)
                    if next_pair is not None:
                        split_gu(*next_pair, s, NF * b + 2 * pair + s + 1)
                    split_act(b, 2 * pair + s, s, P)

            for s in range(2):
                split_gu(0, 0, s, 0)
            act.wait_ge(rest_in, 16)
            hi(gu_rest_hi[:], gu_rest_raw[:]).then_inc(rest_hi_ready, 1)
            for t in range(TB):
                split_h(t)
            act.wait_ge(scales_in, 16 * 5)
            for pair in range(FULL // 2):
                hidden_pair(0, pair, (0, pair + 1) if pair < FULL // 2 - 1 else (1, 0))
                if pair == 0:
                    for t in range(TB, NT):
                        split_h(t)
                else:
                    split_down(pair - 1, P, 2)
            split_down(FULL // 2 - 1, P, 2)
            split_down(FULL // 2, REST, 1)
            gate(0, FULL, 0, bank[6], REST)
            split_act(0, FULL, 0, REST)
            with act.Fori(0, FULL // 2 - 1) as pair:
                hidden_pair(1, pair, (1, pair + 1))
            hidden_pair(1, FULL // 2 - 1, None)
            gate(1, FULL, 0, bank[6], REST)
            split_act(1, FULL, 0, REST)

        @block.vector
        def _(dve):
            def lo(dst, src, hi):
                return nc.vector.tensor_tensor(dst, src, f32(hi), ALU.subtract)

            def tile_squares(tile, squares=qk, slot=0):
                dve.wait_ge(sq_ready, tile + 1)
                nc.vector.tensor_reduce(sq_sum[:, slot, :], squares[:], AX_X, ALU.add).then_inc(sq_sum_ready, 1)

            def q_norm_tile(tile, dst, from_q, slot):
                dve.wait_ge(rstd_ready, tile + 1)
                nc.vector.tensor_tensor(dst[:, 0:GROUP, :], from_q[:].rearrange("p (i d) -> p i d", i=GROUP),
                                        rstd[:, slot, 0:GROUP].unsqueeze(2).broadcast_to([P, GROUP, HD]), ALU.mult)

            def k_norm_tile(dst, from_k, slot):
                nc.vector.tensor_scalar(dst[:, GROUP, :], from_k, rstd[:, slot, GROUP:GROUP + 1], None, ALU.mult).then_inc(normed, 1)

            def tile_v(b, n, from_v):
                lo(v_lo[:, b, n, :], from_v, v_hi[:, b, n, :]).then_inc(v_ready, 1)

            def tile_norm(tile, b, n):
                q_norm_tile(tile, qk, q_bank, 0)
                dve.wait_ge(v_hi_ready, tile + 1)
                k_norm_tile(qk, kv_bank[:, 0:HD], 0)
                tile_v(b, n, kv_bank[:, HD:KVW])

            def tile_qT(tile, b, n, from_q):
                dve.wait_ge(qT_hi_ready, tile + 1)
                q = slice(n * P, (n + 1) * P)
                lo(qT_lo[:, b, :, q], from_q[:].rearrange("p (i q) -> p i q", i=GROUP), qT_hi[:, b, :, q]).then_inc(qT_ready, 1)

            def tile_kT(tile, b, n, from_k, tiles=1):
                dve.wait_ge(kT_hi_ready, tile + tiles)
                dst, leading = (a[:, b, n * P:(n + tiles) * P].rearrange("p (t q) -> p t q", t=tiles) for a in (kT_lo, kT_hi))
                nc.vector.scalar_tensor_tensor(dst, from_k, k_scale, f32(leading), ALU.mult, ALU.subtract).then_inc(kT_ready, tiles)

            def tile_qkT(tile, b, n):
                tile_qT(tile, b, n, tr_bank[1])
                tile_kT(tile, b, n, kv_bank[:, KVW:KVW + P].unsqueeze(1))

            def add_bias(k, n, i):
                wait_apart(dve, scores_done, 4 * k + i + 1)
                nc.vector.tensor_tensor_reduce(out=probs[:, COL[i]:COL[i] + WIDTH[i]], in0=score_bank[i % 2][:, 0:WIDTH[i]],
                                               in1=neg_bias[:, n, SEQ - WIDTH[i]:SEQ], scale=1.0, scalar=HUGE,
                                               op0=ALU.add, op1=ALU.min, accum_out=neg_max[:, i:i + 1]).then_inc(biased, 1)

            def invert(k, part):
                blocks = (slice(0, 2), slice(2, 3), slice(3, 4))[part]
                dve.wait_ge(exp_done, 4 * k + blocks.stop)
                nc.vector.reciprocal(row_sum[:, blocks], row_sum[:, blocks]).then_inc(inv_ready, 1)

            def norm_widest(k):
                dve.wait_ge(inv_ready, 3 * k + 3)
                cols = probs[:, COL[3]:COL[3] + WIDTH[3]]
                nc.vector.tensor_scalar(cols, cols, row_sum[:, 3:4], None, ALU.mult).then_inc(probs3_ready, 1)

            def split_kv(g, c, chunks):
                dve.wait_ge(kvw_hi_ready, NC * g + c + chunks)
                lo(wkv_lo[:, c:c + chunks, :].rearrange("p c n -> p (c n)"), stage_kv[:, c * KVW:(c + chunks) * KVW],
                   wkv_hi[:, c:c + chunks, :].rearrange("p c n -> p (c n)")).then_inc(kvw_ready, chunks)

            def split_q(g, c, chunks):
                dve.wait_ge(qw_hi_ready, NC * g + c + chunks)
                lo(wq_lo[:, c:c + chunks, :].rearrange("p c n -> p (c n)"), stage_q[:, c * QW:(c + chunks) * QW],
                   wq_hi[:, c:c + chunks, :].rearrange("p c n -> p (c n)")).then_inc(qw_ready, chunks)

            def add_attention(tile, t, from_bank=wo_bank):
                dve.wait_ge(wo_done, tile + 1)
                nc.vector.tensor_tensor(h[:, t, :], from_bank[:], h[:, t, :], ALU.add).then_inc(added, 1)

            def split_pT(k, nth, which, src):
                dve.wait_ge(pT_hi_ready, 3 * k + nth + 1)
                cols = slice(BANK_COL[which], BANK_COL[which] + BANK_WIDTH[which])
                lo(pT_lo[:, cols], src[:, 0:BANK_WIDTH[which]], pT_hi[:, cols]).then_inc(pT_ready, 1)

            def statistics(tile, s, src):
                nc.vector.bn_stats(ln_stats[:, s, :], src).then_inc(stats_ready, 1)
                dve.wait_ge(stats_ready, tile + 1)
                nc.vector.bn_aggr(ln_mean_var[:, s, :], ln_stats[:, s, :]).then_inc(var_ready, 1)

            def normalize(tile, s, dst, src):
                dve.wait_ge(ln_rstd_ready, tile + 1)
                return nc.vector.tensor_scalar(dst, src, ln_mean_var[:, s, 0:1], ln_rstd[:, s, :], ALU.subtract, ALU.mult)

            def scan(step):
                dve.wait_ge(scan_in, 16 * step + 16)
                nc.vector.tensor_reduce(scan_max[:, bass.ds(step, 1)], scan_raw[:], AX_X, ALU.max, apply_absolute_value=True).then_inc(scanned, 1)

            def h_statistics(t):
                dve.wait_ge(added, TILES - NT + t + 1)
                statistics(t, t % 2, h[:, t, :])

            def h_normalize(t):
                normalize(t, t % 2, h[:, t, :], h[:, t, :]).then_inc(ln_done, 1)

            def group(g, first, last):
                for b in range(BATCH):
                    for n in range(GROUP):
                        k = 8 * g + 4 * b + n
                        has_next = has_tile(last, b, n)
                        has_prev = not (first and b == 0)
                        has_scores = not (last and b == 1 and n == GROUP - 1)
                        new_weights = b == 0 and n == 2 and not last
                        short = is_short(first, last, b, n)

                        def next_bias(*blocks):
                            for i in blocks if has_scores else ():
                                add_bias(k + 1, (n + 1) % GROUP, i)

                        def next_inverse(part):
                            if has_scores:
                                invert(k + 1, part)

                        def next_probs():
                            if has_scores:
                                invert(k + 1, 2)
                                norm_widest(k + 1)

                        def wait_for_bias():
                            if has_scores:
                                if b == 1 and n == 3:
                                    dve.wait_ge(bias_ready, 4 * g + 5)
                                elif b == 0 and n < 3:
                                    dve.wait_ge(bias_ready, 4 * g + n + 2)
                                dve.wait_ge(pT_done, 3 * k + 3)

                        if short:
                            wait_for_bias()
                            next_bias(0, 1)
                        for nth, which in enumerate(pT_order(first, last, b, n)):
                            if nth == 2 and has_next and not short:
                                tile_squares(k + LEAD)
                            split_pT(k, nth, which, pT_bank(which, first, last, b, n))
                        if short:
                            next_inverse(0)
                            if has_next:
                                tile_squares(k + LEAD)
                            next_bias(2, 3)
                            next_inverse(1)
                        else:
                            wait_for_bias()
                            next_bias(0, 1, 2)
                            next_inverse(0)
                        if has_next:
                            tile_norm(k + LEAD, tile_row(b, n), (n + 1) % TB)
                        if short:
                            next_probs()
                        else:
                            next_bias(3)
                            next_inverse(1)
                        if b == 0 and n == 3 and last:
                            dve.wait_ge(wow_hi_ready, KV_HEADS)
                            lo(wo_lo[:].rearrange("p c n -> p (c n)"), stage_q,
                               wo_hi[:].rearrange("p c n -> p (c n)")).then_inc(wow_ready, 1)
                        dve.wait_ge(oT_hi_ready, k + 1)
                        lo(oT_lo[:, b, n, :], o_bank[:], oT_hi[:, b, n, :]).then_inc(oT_ready, 1)
                        if not short:
                            next_probs()
                        if new_weights and not short:
                            split_q(g + 1, 0, 1)
                        if has_next:
                            tile_qkT(k + LEAD, tile_row(b, n), (n + 1) % TB)
                        if new_weights:
                            if short:
                                split_kv(g + 1, 0, NC)
                                split_q(g + 1, 0, 1)
                            split_q(g + 1, 1, 3)
                        if has_prev:
                            add_attention(k - 4, TB * (1 - b) + n)
                        scan(k)
                        if last and b == 1:
                            h_statistics(n)
                            if n > 0:
                                h_normalize(n - 1)

            raw = h[:].rearrange("p t d -> p (t d)").rearrange("p (c b q) -> p c b q", c=NC, b=BATCH)
            for b in range(BATCH):
                for c in range(NC):
                    dve.wait_ge(xT_hi_ready, NC * b + c + 1)
                    tok = slice(SEQ * b, SEQ * (b + 1))
                    lo(xT_lo[:, c, tok], raw[:, c, b, :], xT_hi[:, c, tok]).then_inc(xT_ready, 1)
                    if b == 0 and c % 2 == 0:
                        split_kv(0, c, 2)
                if b == 0:
                    dve.wait_ge(norm_in, 32)
                    nc.vector.scalar_tensor_tensor(k_scale, norm_w[:, 0:1], -SCALE, norm_w[:, 1:2],
                                                   ALU.mult, ALU.mult).then_inc(k_scale_ready, 1)
                    split_q(0, 0, 2)
                    split_q(0, 2, 2)

            def first_norm(n):
                q_norm_tile(n, first_qk[n], first_q[n], n)
                dve.wait_ge(v_hi_ready, (n | 1) + 1)
                k_norm_tile(first_qk[n], first_k[n], n)
                tile_v(0, n, first_v[n])

            tile_squares(0, first_qk[0], 0)
            tile_squares(1, first_qk[1], 1)
            first_norm(0)
            tile_squares(2, first_qk[2], 2)
            first_norm(1)
            first_norm(2)
            tile_squares(3, first_qk[3], 3)
            for n in range(2):
                tile_qT(n, 0, n, first_q[n])
            dve.wait_ge(k_scale_ready, 1)
            tile_kT(0, 0, 0, first_kT[0], 2)
            first_norm(3)
            tile_qT(2, 0, 2, first_q[2])
            tile_squares(TB)
            tile_qT(3, 0, 3, first_q[3])
            tile_kT(2, 0, 2, first_kT[1], 2)
            dve.wait_ge(bias_ready, GROUP)
            add_bias(0, 0, 0)
            add_bias(0, 0, 1)
            add_bias(0, 0, 2)
            invert(0, 0)
            add_bias(0, 0, 3)
            invert(0, 1)
            tile_norm(TB, 1, 0)
            invert(0, 2)
            norm_widest(0)
            tile_qkT(TB, 1, 0)
            dve.wait_ge(x_in, 16)
            group(0, True, False)
            with dve.Fori(1, KV_HEADS - 1) as g:
                group(g, False, False)
            group(KV_HEADS - 1, False, True)

            def split_gu(b, pair, s):
                dve.wait_ge(gu_hi_ready, FULL * b + 2 * pair + s + 1)
                lo(gu_lo[s][:].rearrange("p a c f -> p (a c f)"), gu_raw[s][:].rearrange("p a c f -> p (a c f)"),
                   gu_hi[s][:].rearrange("p a c f -> p (a c f)")).then_inc(gu_ready, 1)

            def split_h(t):
                dve.wait_ge(hT_hi_ready, t + 1)
                tok = slice(t * P, (t + 1) * P)
                lo(hT_lo[:, :, tok], h_bank[t][:].rearrange("p (c q) -> p c q", c=NC), hT_hi[:, :, tok]).then_inc(hT_ready, 1)

            def split_down(pair, rows, chunks):
                dve.wait_ge(down_hi_ready, pair + 1)
                lo(*(a[0:rows, bass.ds(2 * pair, chunks), :].rearrange("p j d -> p (j d)")
                     for a in (down_lo, down_raw, down_hi))).then_inc(down_ready, 1)

            def gate(b, j, s, up_bank, rows):
                dve.wait_ge(silu_ready, NF * b + j + 1)
                dve.wait_ge(up_done, NF * b + j + 1)
                nc.vector.scalar_tensor_tensor(gated[s][0:rows, :], up_bank[0:rows, :], up_scale[0:rows, bass.ds(j, 1)],
                                               silu[s][0:rows, :], ALU.mult, ALU.mult).then_inc(gated_ready, 1)

            def split_act(b, j, s, rows):
                dve.wait_ge(act_hi_ready, NF * b + j + 1)
                part = bass.ds(j, 1)
                lo(act_lo[0:rows, part, :].rearrange("p j q -> p (j q)"), gated[s][0:rows, :],
                   act_hi[0:rows, part, :].rearrange("p j q -> p (j q)")).then_inc(act_ready, 1)

            def hidden_pair(b, pair, next_pair):
                for s in range(2):
                    gate(b, 2 * pair + s, s, bank[2 + s], P)
                    if next_pair is not None:
                        split_gu(*next_pair, s)
                    split_act(b, 2 * pair + s, s, P)

            def output(b):
                if b > 0:
                    dve.wait_ge(y_out, 16 * TB)
                for n in range(TB):
                    tile = TB * b + n
                    dve.wait_ge(y_done, tile + 1)
                    nc.vector.tensor_tensor(y[n], y_bank[n % 2][:], down_scale[:], ALU.mult).then_inc(y_scaled, 1)
                    dve.wait_ge(y_scaled, tile + 1)
                    nc.vector.tensor_tensor(y[n], y[n], h[:, tile, :], ALU.add).then_inc(y_added, 1)
                    dve.wait_ge(y_added, tile + 1)
                    statistics(NT + tile, n % 2, y[n])
                    normalize(NT + tile, n % 2, y[n], y[n]).then_inc(y_ready, 1)

            h_normalize(TB - 1)
            dve.wait_ge(scanned, STEPS)
            nc.vector.tensor_reduce(row_max[:], scan_max[:], AX_X, ALU.max).then_inc(row_max_ready, 1)
            for s in range(2):
                split_gu(0, 0, s)
            add_attention(TILES - 4, TB, tail_bank[0])
            h_statistics(TB)
            for t in range(TB - 1):
                split_h(t)
            dve.wait_ge(row_max_done, 1)
            nc.vector.tensor_reduce(weight_max[:], score_bank[0][0:1, 0:P], AX_X, ALU.max).then_inc(weight_max_ready, 1)
            dve.wait_ge(weight_max_ready, 1)
            nc.vector.tensor_scalar(narrow[:], weight_max[:], NARROW, None, ALU.is_le).then_inc(narrow_ready, 1)
            add_attention(TILES - 3, TB + 1, tail_bank[1])
            h_statistics(TB + 1)
            h_normalize(TB)
            split_h(TB - 1)
            for n in range(2, GROUP):
                add_attention(TILES - 4 + n, TB + n, tail_bank[n % 2])
                h_statistics(TB + n)
                h_normalize(TB + n - 1)
            dve.wait_ge(rest_hi_ready, 1)
            lo(gu_rest_lo[:].rearrange("p a c f -> p (a c f)"), gu_rest_raw[:].rearrange("p a c f -> p (a c f)"),
               gu_rest_hi[:].rearrange("p a c f -> p (a c f)")).then_inc(rest_ready, 1)
            h_normalize(NT - 1)
            dve.wait_ge(scales_in, 16 * 5)
            hidden_pair(0, 0, (0, 1))
            for t in range(TB, NT):
                split_h(t)
            with dve.Fori(1, FULL // 2 - 1) as pair:
                hidden_pair(0, pair, (0, pair + 1))
                split_down(pair - 1, P, 2)
            hidden_pair(0, FULL // 2 - 1, (1, 0))
            for pair in range(FULL // 2 - 2, FULL // 2):
                split_down(pair, P, 2)
            split_down(FULL // 2, REST, 1)
            gate(0, FULL, 0, bank[7], REST)
            split_act(0, FULL, 0, REST)
            output(0)
            with dve.Fori(0, FULL // 2 - 1) as pair:
                hidden_pair(1, pair, (1, pair + 1))
            hidden_pair(1, FULL // 2 - 1, None)
            gate(1, FULL, 0, bank[7], REST)
            split_act(1, FULL, 0, REST)
            output(1)

        @block.gpsimd
        def _(pool):
            nc.gpsimd.memset(minus_half[:], -0.5).then_inc(consts, 1)
            nc.gpsimd.memset(rms_eps[:], RMS_EPS * HD).then_inc(consts_made, 1)
            nc.gpsimd.memset(ident[:], 1.0).then_inc(consts_made, 1)
            pool.wait_ge(consts_made, 2)
            nc.gpsimd.affine_select(ident[:], ident[:], pattern=[[-1, P]], compare_op=ALU.is_equal, fill=0.0,
                                    base=0, channel_multiplier=1).then_inc(consts, 1)

            def lo(dst, src, hi):
                return nc.gpsimd.tensor_tensor(dst, src, f32(hi), ALU.subtract)

            def split_kv(g):
                pool.wait_ge(kvw_hi_ready, NC * (g + 1))
                lo(wkv_lo[:].rearrange("p c n -> p (c n)"), stage_kv,
                   wkv_hi[:].rearrange("p c n -> p (c n)")).then_inc(kvw_ready, NC)

            def split_o(g):
                pool.wait_ge(wow_hi_ready, g + 1)
                lo(wo_lo[:].rearrange("p c n -> p (c n)"), stage_q,
                   wo_hi[:].rearrange("p c n -> p (c n)")).then_inc(wow_ready, 1)

            def tile_rstd(tile, slot=0):
                pool.wait_ge(sq_sum_ready, tile + 1)
                nc.gpsimd.tensor_tensor(sq_sum[:, slot, :], sq_sum[:, slot, :], rms_eps[:], ALU.add).then_inc(mean_ready, 1)
                pool.wait_ge(mean_ready, tile + 1)
                nc.gpsimd.tensor_tensor(rstd[:, slot, :], sq_sum[:, slot, :], minus_half[:, 0:GROUP + 1], ALU.pow).then_inc(rstd_ready, 1)

            def norm_probs(k, i):
                wait_apart(pool, inv_ready, 3 * k + 1 + i // 2)
                cols = probs[:, COL[i]:COL[i] + WIDTH[i]]
                nc.gpsimd.tensor_scalar(cols, cols, row_sum[:, i:i + 1], 0.0, ALU.mult, ALU.add).then_inc(probs_ready, 1)

            def layer_rstd(tile, s):
                wait_apart(pool, var_ready, tile + 1)
                nc.gpsimd.tensor_scalar(ln_var_eps[:, s, :], ln_mean_var[:, s, 1:2], 1.0, LN_EPS, ALU.mult, ALU.add).then_inc(var_eps_ready, 1)
                pool.wait_ge(var_eps_ready, tile + 1)
                nc.gpsimd.tensor_tensor(ln_rstd[:, s, :], ln_var_eps[:, s, :], minus_half[:, 0:1], ALU.pow).then_inc(ln_rstd_ready, 1)

            def group(g, first, last):
                for b in range(BATCH):
                    for n in range(GROUP):
                        k = 8 * g + 4 * b + n
                        has_next = has_tile(last, b, n)
                        has_scores = not (last and b == 1 and n == GROUP - 1)
                        short = is_short(first, last, b, n)
                        if has_next and not short:
                            tile_rstd(k + LEAD)
                        if b == 0 and n == 2 and not last and not short:
                            split_kv(g + 1)
                        for i in range(2) if has_scores else ():
                            norm_probs(k + 1, i)
                        if has_next and short:
                            tile_rstd(k + LEAD)
                        if has_scores:
                            norm_probs(k + 1, 2)
                        if b == 1 and not last:
                            wait_apart(pool, biased, 4 * k + 4)
                            nc.gpsimd.tensor_scalar(neg_bias[:, n, :], neg_bias[:, n, :], 0.5, 0.0, ALU.mult, ALU.add).then_inc(bias_ready, 1)
                        if b == 0 and n == 3 and not last:
                            split_o(g)
                        if last and b == 1:
                            layer_rstd(n, n % 2)

            for i in range(GROUP):
                bias = neg_bias[:, i, :]
                nc.gpsimd.iota(bias, [[-1, SEQ]], base=SEQ - P, channel_multiplier=1,
                               allow_small_or_imprecise_dtypes=True).then_inc(consts_made, 1)
                pool.wait_ge(consts_made, 2 * i + 3)
                nc.gpsimd.tensor_scalar(bias, bias, SLOPES[i], None, ALU.mult).then_inc(consts_made, 1)
                pool.wait_ge(consts_made, 2 * i + 4)
                nc.gpsimd.affine_select(bias, bias, pattern=[[-1, SEQ]], compare_op=ALU.is_ge, fill=MASKED,
                                        base=SEQ - P, channel_multiplier=1).then_inc(bias_ready, 1)
            for n in range(TB + 1):
                tile_rstd(n, n % TB)
            for i in range(3):
                norm_probs(0, i)
            group(0, True, False)
            with pool.Fori(1, KV_HEADS - 1) as g:
                group(g, False, False)

            group(KV_HEADS - 1, False, True)
            for t in range(TB, NT):
                layer_rstd(t, t % 2)
            with pool.Fori(0, NT // 2) as pair:
                for s in range(2):
                    layer_rstd(NT + 2 * pair + s, s)


def kernel(L0_attn_x, L0_attn_Wq, L0_attn_Wk, L0_attn_Wv, L0_attn_Wo, L0_attn_q_norm_w, L0_attn_k_norm_w,
           L0_ffn_gate_w, L0_ffn_gate_s, L0_ffn_up_w, L0_ffn_up_s, L0_ffn_down_w, L0_ffn_down_s):
    import numpy as np
    import concourse.bacc as bacc
    from concourse.bass_utils import run_bass_kernel_spmd

    def chunked(w, groups):
        w = np.asarray(w).reshape(groups, -1, NC, P)
        return np.ascontiguousarray(w.transpose(0, 3, 2, 1)).reshape(groups, P, -1)

    def hidden_rows(gate, up):
        both = np.stack([gate, up]).reshape(2, -1, min(P, gate.shape[0]), NC, P)
        return np.ascontiguousarray(both.transpose(1, 4, 0, 3, 2)).reshape(both.shape[1], P, -1)

    x = np.asarray(L0_attn_x).reshape(TOK, DM)
    wk = np.asarray(L0_attn_Wk).reshape(KV_HEADS, HD, DM)
    wv = np.asarray(L0_attn_Wv).reshape(KV_HEADS, HD, DM)
    wo = np.asarray(L0_attn_Wo).reshape(DM, KV_HEADS, GROUP, HD)
    gate, up, down = (np.asarray(a) for a in (L0_ffn_gate_w, L0_ffn_up_w, L0_ffn_down_w))
    gate_s, up_s = np.asarray(L0_ffn_gate_s), np.asarray(L0_ffn_up_s)
    arrays = {
        "xT": np.ascontiguousarray(x.reshape(TOK, NC, P).transpose(2, 1, 0)).reshape(P, NC * TOK),
        "x": x,
        "wq": chunked(L0_attn_Wq, KV_HEADS),
        "wkv": chunked(np.concatenate([wk, wv], axis=1), KV_HEADS),
        "wo": np.ascontiguousarray(wo.transpose(1, 3, 2, 0)).reshape(KV_HEADS, HD, GROUP * DM),
        "q_norm": np.asarray(L0_attn_q_norm_w).reshape(HD, 1),
        "k_norm": np.asarray(L0_attn_k_norm_w).reshape(HD, 1),
        "gate_up": hidden_rows(gate[:FULL * P], up[:FULL * P]),
        "gate_up_rest": hidden_rows(gate[FULL * P:], up[FULL * P:])[0],
        "down": np.ascontiguousarray(down[:, :FULL * P].T).reshape(FULL, P, DM),
        "down_rest": np.ascontiguousarray(down[:, FULL * P:].T),
        "gate_s": np.ascontiguousarray(gate_s[:FULL * P].reshape(FULL, P).T),
        "gate_s_rest": gate_s[FULL * P:].reshape(REST, 1),
        "up_s": np.ascontiguousarray(up_s[:FULL * P].reshape(FULL, P).T),
        "up_s_rest": up_s[FULL * P:].reshape(REST, 1),
        "down_s": np.asarray(L0_ffn_down_s),
        "ffn_weights": np.stack([gate, up, down.reshape(gate.shape)]).reshape(STEPS, P, SCAN),
    }
    arrays = {name: np.ascontiguousarray(a) for name, a in arrays.items()}
    nc = bacc.Bacc("TRN2", target_bir_lowering=False, num_devices=1)
    ins = [nc.dram_tensor(name, a.shape, mybir.dt.from_np(a.dtype), kind="ExternalInput").ap() for name, a in arrays.items()]
    out = nc.dram_tensor("out", (NT, P, DM), F32, kind="ExternalOutput").ap()
    block_kernel(nc, *ins, out)
    result = run_bass_kernel_spmd(nc, [arrays], core_ids=[0])
    return result.results[0]["out"].reshape(BATCH, SEQ, DM)
```
